# Optimizing a Trainium2 kernel written in Bass

```python
import numpy as np
import jax
import jax.numpy as jnp

def _softmax(x, axis=-1):
    return jax.nn.softmax(x, axis=axis)

def _gelu(x):
    return jax.nn.gelu(x, approximate=True)

def _silu(x):
    return jax.nn.silu(x)

def _sigmoid(x):
    return jax.nn.sigmoid(x)

def _layernorm(x, axis=-1, eps=1e-05):
    m = jnp.mean(x, axis=axis, keepdims=True)
    v = jnp.var(x, axis=axis, keepdims=True)
    return (x - m) / jnp.sqrt(v + eps)

def _scatter_add(tgt, idx, src, axis=0):
    return tgt.at[idx].add(src)

def _segment_sum(src, seg, n):
    return jax.ops.segment_sum(src, seg, n)
kernel_name = 'mk_adj_resnorm_d4_adj_r2_9ef161'

def setup_inputs(seed: int=0):
    np.random.seed(seed)
    _w = jnp.asarray

    def _rec_inputs():
        import jax
        import jax.numpy as jnp
        _gk = jax.random.key(seed)
        x = -0.0004039 + 1 * jax.random.normal(jax.random.fold_in(_gk, 1), (64, 128, 384), jnp.float32)
        _a = jax.random.bernoulli(jax.random.fold_in(_gk, 2), 0.125, (64, 128, 128))
        _af = _a.astype(jnp.float32)
        adj = _af
        return (x, adj)
    x, adj = _rec_inputs()

    def _L0_gnn_setup():
        import jax, jax.numpy as jnp
        import numpy as np
        B, L, H = (8, 1024, 384)
        LN_EPS = 1e-12
        key = jax.random.key(seed)
        ks = jax.random.split(key, 10)
        hidden_state = jax.random.normal(ks[0], (B, L, H), dtype=jnp.float32)
        adjacency = jax.random.randint(ks[1], (B, L, L), 0, 2).astype(jnp.float32)
        bound = 1.0 / np.sqrt(H)
        W_left = jax.random.normal(ks[2], (H, H), dtype=jnp.float32) * np.sqrt(2.0 / (H + H))
        b_left = jax.random.uniform(ks[3], (H,), minval=-bound, maxval=bound, dtype=jnp.float32)
        W_self = jax.random.normal(ks[4], (H, H), dtype=jnp.float32) * np.sqrt(2.0 / (H + H))
        b_self = jax.random.uniform(ks[5], (H,), minval=-bound, maxval=bound, dtype=jnp.float32)
        W_right = jax.random.normal(ks[6], (H, H), dtype=jnp.float32) * np.sqrt(2.0 / (H + H))
        b_right = jax.random.uniform(ks[7], (H,), minval=-bound, maxval=bound, dtype=jnp.float32)
        gamma = jnp.ones((H,), dtype=jnp.float32)
        beta = jnp.zeros((H,), dtype=jnp.float32)
        return {'hidden_state': hidden_state, 'adjacency': adjacency, 'W_left': W_left, 'b_left': b_left, 'W_self': W_self, 'b_self': b_self, 'W_right': W_right, 'b_right': b_right, 'gamma': gamma, 'beta': beta}
    _L0_gnn_all = _L0_gnn_setup()
    _L0_gnn_in = {k: v for k, v in _L0_gnn_all.items() if k in ('W_left', 'b_left', 'W_self', 'b_self', 'W_right', 'b_right', 'gamma', 'beta')}
    del _L0_gnn_all

    def _L1_gnn_setup():
        import jax, jax.numpy as jnp
        import numpy as np
        NUM_HEADS = 12
        HIDDEN = 384
        HEAD = HIDDEN // NUM_HEADS
        SCALE = HIDDEN ** (-0.5)
        key = jax.random.key(seed)
        ks = jax.random.split(key, 8)
        B, N = (16, 256)
        std = HIDDEN ** (-0.5)
        return {'x': jax.random.normal(ks[0], (B, N, HIDDEN), dtype=jnp.float32), 'encoding_bias': jax.random.normal(ks[1], (B, N, N), dtype=jnp.float32), 'Wq': jax.random.normal(ks[2], (HIDDEN, HIDDEN), dtype=jnp.float32) * std, 'Wk': jax.random.normal(ks[3], (HIDDEN, HIDDEN), dtype=jnp.float32) * std, 'Wv': jax.random.normal(ks[4], (HIDDEN, HIDDEN), dtype=jnp.float32) * std, 'bv': jax.random.normal(ks[5], (HIDDEN,), dtype=jnp.float32) * 0.01, 'Wo': jax.random.normal(ks[6], (HIDDEN, HIDDEN), dtype=jnp.float32) * std, 'bo': jax.random.normal(ks[7], (HIDDEN,), dtype=jnp.float32) * 0.01}
    _L1_gnn_all = _L1_gnn_setup()
    _L1_gnn_in = {k: v for k, v in _L1_gnn_all.items() if k in ('Wq', 'Wk', 'Wv', 'bv', 'Wo', 'bo')}
    del _L1_gnn_all

    def _L2_gnn_setup():
        import jax, jax.numpy as jnp
        import numpy as np
        B, S, H, L = (32, 256, 384, 2)

        def _layer_norm(z, a, b, eps=0.001):
            mu = jnp.mean(z, axis=-1, keepdims=True)
            sigma = jnp.std(z, axis=-1, keepdims=True, ddof=1)
            return (z - mu) / (sigma + eps) * a + b
        key = jax.random.key(seed)
        ks = jax.random.split(key, 6)
        hidden_state = jax.random.normal(ks[0], (B, S, H), dtype=jnp.float32)
        adjacency_matrix = (jax.random.uniform(ks[1], (B, S, S)) < 0.2).astype(jnp.float32)
        W_left = 0.05 * jax.random.normal(ks[2], (L, H, H), dtype=jnp.float32)
        W_right = 0.05 * jax.random.normal(ks[3], (L, H, H), dtype=jnp.float32)
        W_lin = 0.05 * jax.random.normal(ks[4], (L, H, H), dtype=jnp.float32)
        b_lin = jnp.zeros((L, H), dtype=jnp.float32)
        ln_a = jnp.ones((L, H), dtype=jnp.float32)
        ln_b = jnp.zeros((L, H), dtype=jnp.float32)
        return {'hidden_state': hidden_state, 'adjacency_matrix': adjacency_matrix, 'W_left': W_left, 'W_right': W_right, 'W_lin': W_lin, 'b_lin': b_lin, 'ln_a': ln_a, 'ln_b': ln_b}
    _L2_gnn_all = _L2_gnn_setup()
    _L2_gnn_in = {k: v for k, v in _L2_gnn_all.items() if k in ('W_left', 'W_right', 'W_lin', 'b_lin', 'ln_a', 'ln_b')}
    del _L2_gnn_all

    def _L3_gnn_setup():
        import jax, jax.numpy as jnp
        import numpy as np
        LN_EPS = 1e-12

        def _digcn_forward(hidden_state, adjacency_matrix, Wl, bl, Ws, bs, Wr, br, ln_w, ln_b):
            B, S, D = hidden_state.shape
            temper = jnp.asarray(D, jnp.float32) ** 0.5
            i = jnp.arange(S)
            upper = (i[None, :] > i[:, None]).astype(hidden_state.dtype)
            lower = (i[None, :] < i[:, None]).astype(hidden_state.dtype)

            def layer(h, params):
                wl, b_l, ws, b_s, wr, b_r, g, beta = params
                u = jnp.einsum('bid,bjd->bij', h, h) / temper
                a = jax.nn.softmax(u, axis=-1)
                delta = a * adjacency_matrix
                attn = delta / (jnp.sum(delta, axis=-1, keepdims=True) + 1e-10)
                hl = h @ wl.T + b_l
                hs = h @ ws.T + b_s
                hr = h @ wr.T + b_r
                diag_a = jnp.diagonal(attn, axis1=1, axis2=2)
                ctx = jnp.einsum('bij,bjd->bid', attn * upper, hl) + diag_a[..., None] * hs + jnp.einsum('bij,bjd->bid', attn * lower, hr)
                mean = ctx.mean(-1, keepdims=True)
                var = ctx.var(-1, keepdims=True)
                o = (ctx - mean) / jnp.sqrt(var + LN_EPS) * g + beta
                return (jax.nn.relu(o), None)
            out, _ = jax.lax.scan(layer, hidden_state, (Wl, bl, Ws, bs, Wr, br, ln_w, ln_b))
            return out
        key = jax.random.key(seed)
        ks = jax.random.split(key, 6)
        B, S, D, L = (8, 512, 384, 2)
        scale = (1.0 / D) ** 0.5
        hidden_state = jax.random.normal(ks[0], (B, S, D), jnp.float32)
        adjacency_matrix = (jax.random.uniform(ks[1], (B, S, S)) < 0.05).astype(jnp.float32)
        Wl = jax.random.normal(ks[2], (L, D, D), jnp.float32) * scale
        Ws = jax.random.normal(ks[3], (L, D, D), jnp.float32) * scale
        Wr = jax.random.normal(ks[4], (L, D, D), jnp.float32) * scale
        bl = jnp.zeros((L, D), jnp.float32)
        bs = jnp.zeros((L, D), jnp.float32)
        br = jnp.zeros((L, D), jnp.float32)
        ln_w = jnp.ones((L, D), jnp.float32)
        ln_b = jnp.zeros((L, D), jnp.float32)
        return dict(hidden_state=hidden_state, adjacency_matrix=adjacency_matrix, Wl=Wl, bl=bl, Ws=Ws, bs=bs, Wr=Wr, br=br, ln_w=ln_w, ln_b=ln_b)
    _L3_gnn_all = _L3_gnn_setup()
    _L3_gnn_in = {k: v for k, v in _L3_gnn_all.items() if k in ('Wl', 'bl', 'Ws', 'bs', 'Wr', 'br', 'ln_w', 'ln_b')}
    del _L3_gnn_all
    return {'x': x, 'adj': adj, 'L0_gnn_W_left': _L0_gnn_in['W_left'], 'L0_gnn_b_left': _L0_gnn_in['b_left'], 'L0_gnn_W_self': _L0_gnn_in['W_self'], 'L0_gnn_b_self': _L0_gnn_in['b_self'], 'L0_gnn_W_right': _L0_gnn_in['W_right'], 'L0_gnn_b_right': _L0_gnn_in['b_right'], 'L0_gnn_gamma': _L0_gnn_in['gamma'], 'L0_gnn_beta': _L0_gnn_in['beta'], 'L1_gnn_Wq': _L1_gnn_in['Wq'], 'L1_gnn_Wk': _L1_gnn_in['Wk'], 'L1_gnn_Wv': _L1_gnn_in['Wv'], 'L1_gnn_bv': _L1_gnn_in['bv'], 'L1_gnn_Wo': _L1_gnn_in['Wo'], 'L1_gnn_bo': _L1_gnn_in['bo'], 'L2_gnn_W_left': _L2_gnn_in['W_left'], 'L2_gnn_W_right': _L2_gnn_in['W_right'], 'L2_gnn_W_lin': _L2_gnn_in['W_lin'], 'L2_gnn_b_lin': _L2_gnn_in['b_lin'], 'L2_gnn_ln_a': _L2_gnn_in['ln_a'], 'L2_gnn_ln_b': _L2_gnn_in['ln_b'], 'L3_gnn_Wl': _L3_gnn_in['Wl'], 'L3_gnn_bl': _L3_gnn_in['bl'], 'L3_gnn_Ws': _L3_gnn_in['Ws'], 'L3_gnn_bs': _L3_gnn_in['bs'], 'L3_gnn_Wr': _L3_gnn_in['Wr'], 'L3_gnn_br': _L3_gnn_in['br'], 'L3_gnn_ln_w': _L3_gnn_in['ln_w'], 'L3_gnn_ln_b': _L3_gnn_in['ln_b']}

def reference(x, adj, L0_gnn_W_left, L0_gnn_b_left, L0_gnn_W_self, L0_gnn_b_self, L0_gnn_W_right, L0_gnn_b_right, L0_gnn_gamma, L0_gnn_beta, L1_gnn_Wq, L1_gnn_Wk, L1_gnn_Wv, L1_gnn_bv, L1_gnn_Wo, L1_gnn_bo, L2_gnn_W_left, L2_gnn_W_right, L2_gnn_W_lin, L2_gnn_b_lin, L2_gnn_ln_a, L2_gnn_ln_b, L3_gnn_Wl, L3_gnn_bl, L3_gnn_Ws, L3_gnn_bs, L3_gnn_Wr, L3_gnn_br, L3_gnn_ln_w, L3_gnn_ln_b):
    import jax
    import jax.numpy as jnp

    def _L0_gnn_ref(hidden_state, adjacency, W_left, b_left, W_self, b_self, W_right, b_right, gamma, beta):
        import jax, jax.numpy as jnp
        import numpy as np
        B, L, H = (8, 1024, 384)
        LN_EPS = 1e-12
        h = hidden_state
        d = h.shape[-1]
        n = h.shape[1]
        u = jnp.einsum('bld,bmd->blm', h, h) / jnp.sqrt(jnp.asarray(d, h.dtype))
        p = jax.nn.softmax(u, axis=-1)
        delta = p * adjacency
        attn = delta / (jnp.sum(delta, axis=2, keepdims=True) + 1e-10)
        h_left = jnp.einsum('bld,ed->ble', h, W_left) + b_left
        h_self = jnp.einsum('bld,ed->ble', h, W_self) + b_self
        h_right = jnp.einsum('bld,ed->ble', h, W_right) + b_right
        i = jnp.arange(n)[:, None]
        j = jnp.arange(n)[None, :]
        attn_left = jnp.where(j > i, attn, 0.0)
        attn_right = jnp.where(j < i, attn, 0.0)
        diag_a = jnp.diagonal(attn, axis1=1, axis2=2)
        ctx = jnp.einsum('blm,bmd->bld', attn_left, h_left) + diag_a[..., None] * h_self + jnp.einsum('blm,bmd->bld', attn_right, h_right)
        mu = jnp.mean(ctx, axis=-1, keepdims=True)
        var = jnp.mean(jnp.square(ctx - mu), axis=-1, keepdims=True)
        o = (ctx - mu) / jnp.sqrt(var + LN_EPS) * gamma + beta
        return jax.nn.relu(o)

    def _L1_gnn_ref(x, encoding_bias, Wq, Wk, Wv, bv, Wo, bo):
        import jax, jax.numpy as jnp
        import numpy as np
        NUM_HEADS = 12
        HIDDEN = 384
        HEAD = HIDDEN // NUM_HEADS
        SCALE = HIDDEN ** (-0.5)
        B, N, _ = x.shape
        q = (x @ Wq.T).reshape(B, N, NUM_HEADS, HEAD)
        k = (x @ Wk.T).reshape(B, N, NUM_HEADS, HEAD)
        v = (x @ Wv.T + bv).reshape(B, N, NUM_HEADS, HEAD)
        a = jnp.einsum('bnhd,bmhd->bhnm', q, k) * SCALE + encoding_bias[:, None, :, :]
        pad_mask = jnp.all(a == 0, axis=-1)
        a = jnp.where(pad_mask[..., None], -jnp.inf, a)
        a = jax.nn.softmax(a, axis=-1)
        a = jnp.nan_to_num(a)
        o = jnp.einsum('bhnm,bmhd->bnhd', a, v).reshape(B, N, HIDDEN)
        return o @ Wo.T + bo

    def _L2_gnn_ref(hidden_state, adjacency_matrix, W_left, W_right, W_lin, b_lin, ln_a, ln_b):
        import jax, jax.numpy as jnp
        import numpy as np
        B, S, H, L = (32, 256, 384, 2)

        def _layer_norm(z, a, b, eps=0.001):
            mu = jnp.mean(z, axis=-1, keepdims=True)
            sigma = jnp.std(z, axis=-1, keepdims=True, ddof=1)
            return (z - mu) / (sigma + eps) * a + b
        temper = float(np.sqrt(H))
        adj = adjacency_matrix
        adj_tri = jnp.triu(adj, k=1)
        diag_mask = jnp.triu(adj, k=0) - adj_tri
        h = hidden_state
        for l in range(L):
            m_left = jnp.einsum('bsh,oh->bso', h, W_left[l])
            m_right = jnp.einsum('bsh,oh->bso', h, W_right[l])
            u_left = jnp.einsum('bih,bjh->bij', h, m_left) / temper
            u_right = jnp.einsum('bih,bjh->bij', h, m_right) / temper
            u = u_left * adj_tri + u_left * diag_mask + u_right * jnp.swapaxes(adj_tri, 1, 2)
            delta_exp_u = jnp.exp(u) * adj
            attention = delta_exp_u / (jnp.sum(delta_exp_u, axis=2, keepdims=True) + 1e-10)
            h_lin = jnp.einsum('bsh,oh->bso', h, W_lin[l]) + b_lin[l]
            ctx = jnp.matmul(attention, h_lin)
            h = jax.nn.relu(_layer_norm(ctx, ln_a[l], ln_b[l]))
        return h

    def _L3_gnn_ref(hidden_state, adjacency_matrix, Wl, bl, Ws, bs, Wr, br, ln_w, ln_b):
        import jax, jax.numpy as jnp
        import numpy as np
        LN_EPS = 1e-12

        def _digcn_forward(hidden_state, adjacency_matrix, Wl, bl, Ws, bs, Wr, br, ln_w, ln_b):
            B, S, D = hidden_state.shape
            temper = jnp.asarray(D, jnp.float32) ** 0.5
            i = jnp.arange(S)
            upper = (i[None, :] > i[:, None]).astype(hidden_state.dtype)
            lower = (i[None, :] < i[:, None]).astype(hidden_state.dtype)

            def layer(h, params):
                wl, b_l, ws, b_s, wr, b_r, g, beta = params
                u = jnp.einsum('bid,bjd->bij', h, h) / temper
                a = jax.nn.softmax(u, axis=-1)
                delta = a * adjacency_matrix
                attn = delta / (jnp.sum(delta, axis=-1, keepdims=True) + 1e-10)
                hl = h @ wl.T + b_l
                hs = h @ ws.T + b_s
                hr = h @ wr.T + b_r
                diag_a = jnp.diagonal(attn, axis1=1, axis2=2)
                ctx = jnp.einsum('bij,bjd->bid', attn * upper, hl) + diag_a[..., None] * hs + jnp.einsum('bij,bjd->bid', attn * lower, hr)
                mean = ctx.mean(-1, keepdims=True)
                var = ctx.var(-1, keepdims=True)
                o = (ctx - mean) / jnp.sqrt(var + LN_EPS) * g + beta
                return (jax.nn.relu(o), None)
            out, _ = jax.lax.scan(layer, hidden_state, (Wl, bl, Ws, bs, Wr, br, ln_w, ln_b))
            return out
        return _digcn_forward(hidden_state, adjacency_matrix, Wl, bl, Ws, bs, Wr, br, ln_w, ln_b)
    x = _layernorm(x + _L0_gnn_ref(x, adj, L0_gnn_W_left, L0_gnn_b_left, L0_gnn_W_self, L0_gnn_b_self, L0_gnn_W_right, L0_gnn_b_right, L0_gnn_gamma, L0_gnn_beta), axis=-1)
    x = _layernorm(x + _L1_gnn_ref(x, adj, L1_gnn_Wq, L1_gnn_Wk, L1_gnn_Wv, L1_gnn_bv, L1_gnn_Wo, L1_gnn_bo), axis=-1)
    x = _layernorm(x + _L2_gnn_ref(x, adj, L2_gnn_W_left, L2_gnn_W_right, L2_gnn_W_lin, L2_gnn_b_lin, L2_gnn_ln_a, L2_gnn_ln_b), axis=-1)
    x = _layernorm(x + _L3_gnn_ref(x, adj, L3_gnn_Wl, L3_gnn_bl, L3_gnn_Ws, L3_gnn_bs, L3_gnn_Wr, L3_gnn_br, L3_gnn_ln_w, L3_gnn_ln_b), axis=-1)
    return x

_drawn_inputs = setup_inputs


def setup_inputs(seed=0):
    import zlib

    import numpy as np

    out = dict(_drawn_inputs(seed))
    spreads = {'L0_gnn_gamma': (1.0, 0.2),
     'L0_gnn_beta': (0.0, 0.1),
     'L2_gnn_b_lin': (0.0, 0.1),
     'L2_gnn_ln_a': (1.0, 0.2),
     'L2_gnn_ln_b': (0.0, 0.1),
     'L3_gnn_bl': (0.0, 0.1),
     'L3_gnn_bs': (0.0, 0.1),
     'L3_gnn_br': (0.0, 0.1),
     'L3_gnn_ln_w': (1.0, 0.2),
     'L3_gnn_ln_b': (0.0, 0.1)}
    factors = {'L0_gnn_b_self': 7.216, 'L1_gnn_bo': 3.004, 'L1_gnn_bv': 2.679}
    for name, (base, spread) in spreads.items():
        noise = np.random.default_rng([zlib.crc32(name.encode()), seed]).standard_normal(out[name].shape)
        drawn = base * np.exp(spread * noise) if base else spread * noise
        out[name] = jnp.asarray(drawn.astype(out[name].dtype))
    for name, factor in factors.items():
        out[name] = (out[name] * factor).astype(out[name].dtype)
    return out
```

```python
import concourse.bass as bass
from concourse import mybir
from contextlib import ExitStack

G, N, D = 64, 128, 384
KT = D // 128
U = 4
HEADS, HEAD = 12, 32
HV = HEAD + 2
NB = 13
NG = 10

fp32 = mybir.dt.float32
fp32r = mybir.dt.float32r
ALU = mybir.AluOpType
ACT = mybir.ActivationFunctionType
AX = mybir.AxisListType

SCALARS = [-0.5, 0.5, 1e-12, 1e-5, float(D) / (D - 1)]
INV_SQRT, SQRT, EPS_INNER, EPS_OUTER, UNBIASED = range(5)


def is_live(K, c):
    return not isinstance(K, int) or 0 <= K + c < G


def steps(eng, body, tail):
    for c in range(-1, U):
        body(0, c)
    with eng.Fori(U, G - 2 * U + 1, U) as K:
        for c in range(U):
            body(K, c)
    for c in range(U + tail):
        body(G - U, c)


def program(nc, x_in, adj_in, w_in, bias_in, gain_in, out, scratch):
    ctx = ExitStack()
    with ctx:
        core = Core(nc, ctx, x_in, adj_in, w_in, bias_in, gain_in)
        setup(core)
        digcn(core, 0, x_in, x_in, scratch[0], bias=0, gain=0, closing=True)
        attention(core, 1, scratch[0], scratch[1])
        exp_gnn(core, 2, scratch[1], None, scratch[2], gain=2, bias=5)
        exp_gnn(core, 3, scratch[2], scratch[1], scratch[3], gain=4, bias=6)
        digcn(core, 4, scratch[3], None, scratch[4], bias=7, gain=6, closing=False)
        digcn(core, 5, scratch[4], scratch[3], out, bias=10, gain=8, closing=True)


WEIGHTS = [(0, 3), (3, 4), (7, 3), (10, 3), (13, 3), (16, 3)]


class Core:

    def __init__(self, nc, ctx, x_in, adj_in, w_in, bias_in, gain_in):
        self.nc, self.ctx, self.sems, self.phases_with = nc, ctx, {}, {}
        self.adj_in, self.w_in, self.bias_in, self.gain_in = adj_in, w_in, bias_in, gain_in
        self.ident = self.sb("ident", [128, 128])
        self.upper = self.sb("upper", [128, 128])
        self.lower = self.sb("lower", [128, 128])
        self.lowtri = self.sb("lowtri", [128, 128])
        self.ones = self.sb("ones", [128, 128], fp32r)
        self.scalars = self.sb("scalars", [128, len(SCALARS)])
        self.bias = self.sb("bias", [128, NB, D], fp32r)
        self.gain = self.sb("gain", [128, NG, D])
        self.w_raw = self.sb("w_raw", [128, 4, KT, D])
        self.w_hi = self.sb("w_hi", [128, 2, 4, KT, D], fp32r)
        self.w_lo = self.sb("w_lo", [128, 2, 4, KT, D], fp32r)
        self.banks = [ctx.enter_context(nc.psum_tensor(f"bank{i}", [128, 512], fp32)) for i in range(8)]

    def scalar(self, k):
        return self.scalars[:, k:k + 1]

    def sb(self, name, shape, dt=fp32):
        return self.ctx.enter_context(self.nc.sbuf_tensor(name, shape, dt))

    def sem(self, name):
        if name not in self.sems:
            self.sems[name] = self.ctx.enter_context(self.nc.semaphore(name))
        return self.sems[name]

    def load_weights(self, sp, n):
        first, count = WEIGHTS[n]
        for m in range(count):
            if n:
                before = [p for p in range(n) if m < WEIGHTS[p][1]]
                if before:
                    sp.wait_ge(self.sem(f"w_lo{m}"), len(before))
            sp.dma_start(self.w_raw[:, m], self.w_in[first + m]).then_inc(self.sem(f"w_loaded{m}"), 16)

    def uses(self, n, m):
        return sum(m < WEIGHTS[p][1] for p in range(n + 1))

    def split_hi(self, act, n, m):
        act.wait_ge(self.sem(f"w_loaded{m}"), 16 * self.uses(n, m))
        act.activation(self.w_hi[:, n % 2, m], self.w_raw[:, m], ACT.Copy).then_inc(self.sem(f"w_hi{m}"), 1)

    def split_lo(self, pool, n, m):
        pool.wait_ge(self.sem(f"w_hi{m}"), self.uses(n, m))
        pool.tensor_tensor(self.w_lo[:, n % 2, m], self.w_raw[:, m],
                           self.w_hi[:, n % 2, m].bitcast(fp32), ALU.subtract).then_inc(self.sem(f"w_lo{m}"), 1)

    def next_split(self, eng, split, n, K, c):
        if isinstance(K, int) and K == G - U and n + 1 < len(WEIGHTS) and 0 <= c < WEIGHTS[n + 1][1]:
            split(eng, n + 1, c)


def setup(core):
    nc = core.nc
    s = core.sem
    with nc.sbuf_tensor("bias_raw", [128, NB, D], fp32) as raw, nc.Block() as block:
        @block.sync
        def _(sp):
            sp.dma_start(raw[:, :, :], core.bias_in.unsqueeze(0).to_broadcast([128, NB, D])).then_inc(s("bias_loaded"), 16)
            core.load_weights(sp, 0)
            sp.dma_start(core.gain[:, :, :], core.gain_in.unsqueeze(0).to_broadcast([128, NG, D])).then_inc(s("gain_loaded"), 16)
            sp.wait_ge(s("gain_loaded"), 16)

        @block.gpsimd
        def _(pool):
            for t in (core.ident, core.upper, core.lower, core.lowtri):
                pool.memset(t[:, :], 0.0 if t is core.ident else 1.0).then_inc(s("consts"), 1)
            pool.wait_ge(s("consts"), 4)
            for t, op, fill in ((core.ident, ALU.not_equal, 1.0), (core.lowtri, ALU.is_ge, 0.0), (core.lower, ALU.is_gt, 0.0)):
                pool.affine_select(out=t[:, :], in_=t[:, :], compare_op=op, fill=fill, base=0,
                                   pattern=[[-1, 128]], channel_multiplier=1).then_inc(s("consts"), 1)
            pool.affine_select(out=core.upper[:, :], in_=core.upper[:, :], compare_op=ALU.is_gt, fill=0.0, base=0,
                               pattern=[[1, 128]], channel_multiplier=-1).then_inc(s("consts"), 1)
            for k, value in enumerate(SCALARS):
                pool.memset(core.scalars[:, k:k + 1], value).then_inc(s("consts"), 1)
            for m in range(WEIGHTS[0][1]):
                core.split_lo(pool, 0, m)

        @block.scalar
        def _(act):
            act.wait_ge(s("bias_loaded"), 16)
            act.activation(core.bias[:, :, :], raw[:, :, :], ACT.Copy).then_inc(s("bias_hi"), 1)
            for m in range(WEIGHTS[0][1]):
                core.split_hi(act, 0, m)

        @block.vector
        def _(dve):
            dve.memset(core.ones[:, :].bitcast(fp32), 1.0).then_inc(s("ones"), 1)
            dve.wait_ge(s("bias_hi"), 1)
            hi = core.bias[:, :, :].bitcast(fp32)
            dve.tensor_tensor(raw[:, :, :], raw[:, :, :], hi, ALU.subtract).then_inc(s("bias_lo"), 1)
            dve.wait_ge(s("consts"), 8 + len(SCALARS))
            dve.wait_ge(s("bias_lo"), 1)
            dve.tensor_scalar(raw[:, :, :], raw[:, :, :], core.ident[:, 1:2], None, ALU.mult).then_inc(s("bias_lo"), 1)
            dve.wait_ge(s("bias_lo"), 2)
            dve.scalar_tensor_tensor(core.bias[:, :, :].rearrange("p a b -> p (a b)"), hi.rearrange("p a b -> p (a b)"),
                                     core.ident[:, 0:1], raw[:, :, :].rearrange("p a b -> p (a b)"),
                                     op0=ALU.mult, op1=ALU.add).then_inc(s("bias_ready"), 1)
            dve.wait_ge(s("bias_ready"), 1)


class Phase:

    def __init__(self, core, n):
        self.core, self.n, self.used = core, n, set()

    def base(self, name):
        if name not in self.used:
            self.used.add(name)
            self.core.phases_with[name] = self.core.phases_with.get(name, 0) + 1
        return G * (self.core.phases_with[name] - 1)

    def sem(self, name):
        self.base(name)
        return self.core.sem(name)

    def upto(self, name, K, c, per=1, extra=0):
        if isinstance(K, int):
            c = min(c, G - 1 - K)
        count = K * per + (self.base(name) + c + 1) * per + extra
        return max(count, 0) if isinstance(K, int) else count

    def moved(self, name, K, c, slots, per):
        count = K * (per // slots) + (self.base(f"{name}{c % slots}") // slots + c // slots + 1) * per
        return max(count, 0) if isinstance(K, int) else count


def mm3(pe, out, lhs, rhs, first, last):
    pe.matmul(out, lhs[0], rhs[0], start=first, stop=False)
    pe.matmul(out, lhs[0], rhs[1], start=False, stop=False)
    return pe.matmul(out, lhs[1], rhs[0], start=False, stop=last)


def tile_of(dram, K, c):
    if isinstance(K, int):
        return dram[K + c]
    return dram[bass.ds(K + c, 1)].rearrange("a p d -> (a p) d")


def io(ph, sp, x_src, x, adj, res_src, res, dst, result, event):
    def body(K, c):
        if is_live(K, c - 4):
            sp.wait_ge(ph.sem(event), ph.upto(event, K, c - 4))
            sp.dma_start(tile_of(dst, K, c - 4), result[:, c % 2]).then_inc(ph.sem(f"stored{c % 2}"), 16)
        if is_live(K, c + 2):
            sp.wait_ge(ph.sem("y"), ph.upto("y", K, c + 2 - U))
            sl = (c + 2) % U
            sp.dma_start(x[:, sl], tile_of(x_src, K, c + 2)).then_inc(ph.sem(f"loaded{sl}"), 16)
            sp.dma_start(adj[:, sl], tile_of(ph.core.adj_in, K, c + 2)).then_inc(ph.sem(f"loaded{sl}"), 16)
            if res_src is not None:
                sp.dma_start(res[:, sl], tile_of(res_src, K, c + 2)).then_inc(ph.sem(f"residual{sl}"), 16)
    body(0, -2)
    steps(sp, body, 4)
    for i in range(2):
        sp.wait_ge(ph.sem(f"stored{i}"), 16 * (ph.base(f"stored{i}") + G) // 2)


def digcn(core, n, x_src, res_src, dst, bias, gain, closing):
    nc = core.nc
    own_res = closing and res_src is not x_src
    ph = Phase(core, n)
    S, T, B = ph.sem, ph.upto, ph.moved
    temper = float(D) ** -0.5
    wh, wl = core.w_hi[:, n % 2], core.w_lo[:, n % 2]
    bT, bS, bL, bR, bH, bE, bC = (core.banks[i] for i in range(7))
    with ExitStack() as lc:
        sb = lambda name, shape, dt=fp32: lc.enter_context(nc.sbuf_tensor(f"{name}_{n}", shape, dt))
        x = sb("x", [128, U, D])
        res = sb("res", [128, U, D]) if own_res else x
        adj = sb("adj", [128, U, N])
        xT = [sb(f"xT{i}", [128, 2, KT, N], fp32r) for i in "hl"]
        hL = [sb(f"hL{i}", [128, 2, D], fp32r) for i in "hl"]
        hR = [sb(f"hR{i}", [128, 2, D], fp32r) for i in "hl"]
        selfp = sb("selfp", [128, 2, D])
        e = sb("e", [128, N])
        delta = sb("delta", [128, 2, N])
        dscr = sb("dscr", [128, N])
        eT = sb("eT", [128, 2, N])
        eTs = [sb(f"eT{i}", [128, 2, N], fp32r) for i in "hl"]
        z = sb("z", [128, 2, D])
        t = sb("t", [128, 2, D])
        y = sb("y", [128, 2, D])
        o = sb("o", [128, 2, D])
        sm = sb("sm", [128, 2, 32])
        MX, NM, ES, DS, RS, RI, DG = range(7)
        ST, AG, VE, RSTD, NMR = 8, 14, 16, 17, 18
        ST2, AG2, VE2, RSTD2, NMR2 = 20, 26, 28, 29, 30

        def col(c, i, w=1):
            return sm[:, c % 2, i:i + w]

        with nc.Block() as block:
            @block.sync
            def _(sp):
                if n + 1 < len(WEIGHTS):
                    core.load_weights(sp, n + 1)

                io(ph, sp, x_src, x, adj, res_src if own_res else None, res, dst,
                   o if closing else y, "o" if closing else "y")

            @block.tensor
            def _(pe):
                for m in range(3):
                    pe.wait_ge(core.sem(f"w_lo{m}"), core.uses(n, m))
                pe.wait_ge(core.sem("bias_ready"), 1)
                pe.wait_ge(core.sem("ones"), 1)

                def project(bank, m, c):
                    pe.matmul(bank[:, 0:D], core.ones[:, :], core.bias[:, bias + m], start=True, stop=False)
                    for kt in range(KT):
                        last = mm3(pe, bank[:, 0:D], [v[:, c % 2, kt] for v in xT],
                                   [wh[:, m, kt], wl[:, m, kt]], False, kt == KT - 1)
                    return last

                def body(K, c):
                    if is_live(K, c):
                        pe.wait_ge(S("xT_lo"), T("xT_lo", K, c))
                        pe.wait_ge(S("exp"), T("exp", K, c - 1))
                        for kt in range(KT):
                            v = [a[:, c % 2, kt] for a in xT]
                            last = mm3(pe, bS[:, 0:N], v, v, kt == 0, kt == KT - 1)
                        last.then_inc(S("scores"), 1)
                        pe.wait_ge(S("hL_lo"), T("hL_lo", K, c - 1))
                        project(bL, 0, c).then_inc(S("hL_ps"), 1)
                    if is_live(K, c - 1):
                        pe.wait_ge(S("delta"), T("delta", K, c - 1))
                        pe.wait_ge(S("eT"), T("eT", K, c - 2))
                        pe.transpose(bE[:, 0:N], delta[:, (c - 1) % 2], core.ident[:, :]).then_inc(S("eT_ps"), 1)
                    if is_live(K, c):
                        pe.wait_ge(S("hR_lo"), T("hR_lo", K, c - 1))
                        project(bR, 2, c).then_inc(S("hR_ps"), 1)
                        pe.wait_ge(S("self"), T("self", K, c - 1))
                        project(bH, 1, c).then_inc(S("self_ps"), 1)
                    if is_live(K, c + 1):
                        pe.wait_ge(S(f"loaded{(c + 1) % U}"), B("loaded", K, c + 1, U, 32))
                        pe.wait_ge(S("xT_lo"), T("xT_lo", K, c))
                        for kt in range(KT):
                            last = pe.transpose(bT[:, kt * N:(kt + 1) * N], x[:, (c + 1) % U, kt * 128:(kt + 1) * 128],
                                                core.ident[:, :])
                        last.then_inc(S("xT_ps"), 1)
                    if is_live(K, c - 1):
                        pe.wait_ge(S("eT_lo"), T("eT_lo", K, c - 1))
                        pe.wait_ge(S("hL_lo"), T("hL_lo", K, c - 1))
                        pe.wait_ge(S("hR_lo"), T("hR_lo", K, c - 1))
                        pe.wait_ge(S("z"), T("z", K, c - 2))
                        mm3(pe, bC[:, 0:D], [v[:, 0] for v in eTs], [v[:, (c - 1) % 2] for v in hL], True, False)
                        mm3(pe, bC[:, 0:D], [v[:, 1] for v in eTs], [v[:, (c - 1) % 2] for v in hR], False, True)\
                            .then_inc(S("ctx"), 1)
                steps(pe, body, 1)

            @block.scalar
            def _(act):
                def body(K, c):
                    core.next_split(act, core.split_hi, n, K, c)
                    if is_live(K, c):
                        act.wait_ge(S("negmax"), T("negmax", K, c))
                        act.activation(e[:, :], bS[:, 0:N], ACT.Exp, bias=col(c, NM), scale=temper,
                                       accum_out=col(c, ES)).then_inc(S("exp"), 1)
                        act.wait_ge(S("hL_ps"), T("hL_ps", K, c))
                        act.activation(hL[0][:, c % 2], bL[:, 0:D], ACT.Copy).then_inc(S("hL_hi"), 1)
                    if is_live(K, c - 1):
                        act.wait_ge(S("eT"), T("eT", K, c - 1))
                        act.activation(eTs[0][:, :, :], eT[:, :, :], ACT.Copy).then_inc(S("eT_hi"), 1)
                    if is_live(K, c - 3) and closing:
                        act.wait_ge(S("nmr2"), T("nmr2", K, c - 3))
                        act.wait_ge(S(f"stored{(c - 5) % 2}"), B("stored", K, c - 5, 2, 16))
                        act.activation(o[:, (c - 3) % 2], y[:, (c - 3) % 2], ACT.Identity, bias=col(c - 3, NMR2),
                                       scale=col(c - 3, RSTD2)).then_inc(S("o"), 1)
                    if is_live(K, c):
                        act.wait_ge(S("hR_ps"), T("hR_ps", K, c))
                        act.activation(hR[0][:, c % 2], bR[:, 0:D], ACT.Copy).then_inc(S("hR_hi"), 1)
                    if is_live(K, c - 2):
                        act.wait_ge(S("nmr"), T("nmr", K, c - 2))
                        act.activation(t[:, (c - 2) % 2], z[:, (c - 2) % 2], ACT.Identity, bias=col(c - 2, NMR),
                                       scale=col(c - 2, RSTD)).then_inc(S("t"), 1)
                    if is_live(K, c):
                        act.wait_ge(S("self_ps"), T("self_ps", K, c))
                        act.wait_ge(S("diag"), T("diag", K, c))
                        act.wait_ge(S("z"), T("z", K, c - 2))
                        act.activation(selfp[:, c % 2], bH[:, 0:D], ACT.Copy, scale=col(c, DG)).then_inc(S("self"), 1)
                    if is_live(K, c + 1):
                        act.wait_ge(S("xT_ps"), T("xT_ps", K, c + 1))
                        act.activation(xT[0][:, (c + 1) % 2], bT[:, 0:D], ACT.Copy).then_inc(S("xT_hi"), 1)

                steps(act, body, 3)

            @block.gpsimd
            def _(pool):
                def body(K, c):
                    core.next_split(pool, core.split_lo, n, K, c)
                    if is_live(K, c - 2):
                        pool.wait_ge(S("agg"), T("agg", K, c - 2))
                        pool.tensor_tensor(col(c - 2, VE), col(c - 2, AG + 1), core.scalar(EPS_INNER), ALU.add).then_inc(S("veps"), 1)
                        pool.wait_ge(S("veps"), T("veps", K, c - 2))
                        pool.tensor_tensor(col(c - 2, RSTD), col(c - 2, VE), core.scalar(INV_SQRT), ALU.pow).then_inc(S("rstd"), 1)
                    if is_live(K, c - 3) and closing:
                        pool.wait_ge(S("agg2"), T("agg2", K, c - 3))
                        pool.tensor_tensor(col(c - 3, VE2), col(c - 3, AG2 + 1), core.scalar(EPS_OUTER), ALU.add).then_inc(S("veps2"), 1)
                        pool.wait_ge(S("veps2"), T("veps2", K, c - 3))
                        pool.tensor_tensor(col(c - 3, RSTD2), col(c - 3, VE2), core.scalar(INV_SQRT), ALU.pow).then_inc(S("rstd2"), 1)
                    if is_live(K, c - 1):
                        pool.wait_ge(S("eT_hi"), T("eT_hi", K, c - 1))
                        pool.tensor_tensor(eTs[1][:, :, :], eT[:, :, :], eTs[0][:, :, :].bitcast(fp32),
                                           ALU.subtract).then_inc(S("eT_lo"), 1)
                    if is_live(K, c - 2):
                        pool.wait_ge(S("t"), T("t", K, c - 2))
                        tt = t[:, (c - 2) % 2]
                        pool.tensor_tensor(tt, tt, core.gain[:, gain], ALU.mult).then_inc(S("gained"), 1)
                        pool.wait_ge(S("gained"), T("gained", K, c - 2))
                        pool.tensor_tensor(tt, tt, core.gain[:, gain + 1], ALU.add).then_inc(S("shifted"), 1)
                steps(pool, body, 3)

            @block.vector
            def _(dve):
                def body(K, c):
                    if is_live(K, c - 2):
                        dve.wait_ge(S("ctx"), T("ctx", K, c - 2))
                        dve.wait_ge(S("self"), T("self", K, c - 2))
                        dve.scalar_tensor_tensor(z[:, (c - 2) % 2], bC[:, 0:D], col(c - 2, RI), selfp[:, (c - 2) % 2],
                                                 op0=ALU.mult, op1=ALU.add).then_inc(S("z"), 1)
                    if is_live(K, c):
                        dve.wait_ge(S("scores"), T("scores", K, c))
                        dve.reduce_max(col(c, MX), bS[:, 0:N], AX.X).then_inc(S("max"), 1)
                    if is_live(K, c - 2):
                        dve.wait_ge(S("z"), T("z", K, c - 2))
                        dve.bn_stats(col(c - 2, ST, 6), z[:, (c - 2) % 2]).then_inc(S("bn"), 1)
                    if is_live(K, c - 2):
                        dve.wait_ge(S("bn"), T("bn", K, c - 2))
                    if is_live(K, c):
                        dve.wait_ge(S("max"), T("max", K, c))
                        dve.tensor_scalar(col(c, NM), col(c, MX), -temper, None, ALU.mult).then_inc(S("negmax"), 1)
                    if is_live(K, c - 2):
                        dve.bn_aggr(col(c - 2, AG, 2), col(c - 2, ST, 6)).then_inc(S("agg"), 1)
                    if is_live(K, c - 3):
                        dve.wait_ge(S("shifted"), T("shifted", K, c - 3))
                        if closing:
                            if own_res:
                                dve.wait_ge(S(f"residual{(c - 3) % U}"), B("residual", K, c - 3, U, 16))
                            dve.scalar_tensor_tensor(y[:, (c - 3) % 2], t[:, (c - 3) % 2], 0.0, res[:, (c - 3) % U],
                                                     op0=ALU.max, op1=ALU.add).then_inc(S("y"), 1)
                        else:
                            dve.wait_ge(S(f"stored{(c - 5) % 2}"), B("stored", K, c - 5, 2, 16))
                            dve.tensor_scalar(y[:, (c - 3) % 2], t[:, (c - 3) % 2], 0.0, None, ALU.max).then_inc(S("y"), 1)
                    if is_live(K, c):
                        dve.wait_ge(S("exp"), T("exp", K, c))
                        dve.wait_ge(S("eT_ps"), T("eT_ps", K, c - 2))
                        dve.scalar_tensor_tensor(delta[:, c % 2], e[:, :], 1.0, adj[:, c % U], op0=ALU.mult,
                                                 op1=ALU.mult, accum_out=col(c, DS)).then_inc(S("delta"), 1)
                    if is_live(K, c - 3) and closing:
                        dve.wait_ge(S("y"), T("y", K, c - 3))
                        dve.bn_stats(col(c - 3, ST2, 6), y[:, (c - 3) % 2]).then_inc(S("bn2"), 1)
                    if is_live(K, c - 3) and closing:
                        dve.wait_ge(S("bn2"), T("bn2", K, c - 3))
                    if is_live(K, c):
                        dve.wait_ge(S("delta"), T("delta", K, c))
                        dve.scalar_tensor_tensor(col(c, RS), col(c, ES), 1e-10, col(c, DS), op0=ALU.mult,
                                                 op1=ALU.add).then_inc(S("rsum"), 1)
                    if is_live(K, c - 3) and closing:
                        dve.bn_aggr(col(c - 3, AG2, 2), col(c - 3, ST2, 6)).then_inc(S("agg2"), 1)
                    if is_live(K, c):
                        dve.wait_ge(S("rsum"), T("rsum", K, c))
                        dve.reciprocal(col(c, RI), col(c, RS)).then_inc(S("rinv"), 1)
                        dve.wait_ge(S("hL_hi"), T("hL_hi", K, c))
                        dve.tensor_tensor(hL[1][:, c % 2], bL[:, 0:D], hL[0][:, c % 2].bitcast(fp32),
                                          ALU.subtract).then_inc(S("hL_lo"), 1)
                    if is_live(K, c - 1):
                        dve.wait_ge(S("eT_ps"), T("eT_ps", K, c - 1))
                        dve.wait_ge(S("eT_lo"), T("eT_lo", K, c - 2))
                        dve.tensor_tensor(eT[:, 0], bE[:, 0:N], core.lower[:, :], ALU.mult).then_inc(S("eT_u"), 1)
                        dve.tensor_tensor(eT[:, 1], bE[:, 0:N], core.upper[:, :], ALU.mult).then_inc(S("eT"), 1)
                    if is_live(K, c - 2):
                        dve.wait_ge(S("rstd"), T("rstd", K, c - 2))
                        dve.scalar_tensor_tensor(col(c - 2, NMR), col(c - 2, AG), -1.0, col(c - 2, RSTD), op0=ALU.mult,
                                                 op1=ALU.mult).then_inc(S("nmr"), 1)
                    if is_live(K, c):
                        dve.wait_ge(S("rinv"), T("rinv", K, c))
                        dve.tensor_tensor_reduce(out=dscr[:, :], in0=delta[:, c % 2], in1=core.ident[:, :],
                                                 scale=col(c, RI), scalar=0.0, op0=ALU.mult, op1=ALU.add,
                                                 accum_out=col(c, DG)).then_inc(S("diag"), 1)
                    if is_live(K, c - 3) and closing:
                        dve.wait_ge(S("rstd2"), T("rstd2", K, c - 3))
                        dve.scalar_tensor_tensor(col(c - 3, NMR2), col(c - 3, AG2), -1.0, col(c - 3, RSTD2), op0=ALU.mult,
                                                 op1=ALU.mult).then_inc(S("nmr2"), 1)
                    if is_live(K, c):
                        dve.wait_ge(S("hR_hi"), T("hR_hi", K, c))
                        dve.tensor_tensor(hR[1][:, c % 2], bR[:, 0:D], hR[0][:, c % 2].bitcast(fp32),
                                          ALU.subtract).then_inc(S("hR_lo"), 1)
                    if is_live(K, c + 1):
                        dve.wait_ge(S("xT_hi"), T("xT_hi", K, c + 1))
                        dve.tensor_tensor(xT[1][:, (c + 1) % 2], bT[:, 0:D], xT[0][:, (c + 1) % 2].bitcast(fp32),
                                          ALU.subtract).then_inc(S("xT_lo"), 1)

                steps(dve, body, 3)


def exp_gnn(core, n, x_src, res_src, dst, gain, bias):
    nc = core.nc
    closing = res_src is not None
    ph = Phase(core, n)
    S, T, B = ph.sem, ph.upto, ph.moved
    temper = float(D) ** -0.5
    wh, wl = core.w_hi[:, n % 2], core.w_lo[:, n % 2]
    bT, bGL, bGR, bH, bU, bA, bC = (core.banks[i] for i in range(7))
    with ExitStack() as lc:
        sb = lambda name, shape, dt=fp32: lc.enter_context(nc.sbuf_tensor(f"{name}_{n}", shape, dt))
        x = sb("x", [128, U, D])
        res = sb("res", [128, U, D]) if closing else None
        adj = sb("adj", [128, U, N])
        xT = [sb(f"xT{i}", [128, 2, KT, N], fp32r) for i in "hl"]
        g = [sb(f"g{i}", [128, KT, 2, N], fp32r) for i in "hl"]
        h = [sb(f"h{i}", [128, 2, D + 2], fp32r) for i in "hl"]
        adjT = sb("adjT", [128, 2, N])
        mask = sb("mask", [128, 2, 2, N])
        w = sb("w", [128, 2, N])
        u = sb("u", [128, N])
        e = sb("e", [128, N])
        ea = sb("ea", [128, N])
        eTs = [sb(f"eT{i}", [128, N], fp32r) for i in "hl"]
        t = sb("t", [128, 2, D])
        y = sb("y", [128, 2, D])
        o = sb("o", [128, 2, D])
        sm = sb("sm", [128, 2, 32])
        ST, AG, RS, RI, VE, SD, DEN, REC, Q, NQ = 0, 6, 8, 9, 10, 11, 12, 13, 14, 15
        ST2, AG2, VE2, RSTD2, NMR2 = 16, 22, 24, 25, 26

        def col(c, i, w=1):
            return sm[:, c % 2, i:i + w]

        with nc.Block() as block:
            @block.sync
            def _(sp):
                if n + 1 < len(WEIGHTS):
                    core.load_weights(sp, n + 1)
                io(ph, sp, x_src, x, adj, res_src, res, dst, o if closing else y, "o" if closing else "y")

            @block.tensor
            def _(pe):
                for m in range(3):
                    pe.wait_ge(core.sem(f"w_lo{m}"), core.uses(n, m))
                pe.wait_ge(core.sem("ones_columns"), n)

                def weighted(bank, m, c):
                    for mt in range(KT):
                        cols = slice(mt * 128, (mt + 1) * 128)
                        for kt in range(KT):
                            last = mm3(pe, bank[:, cols], [wh[:, m, kt, cols], wl[:, m, kt, cols]],
                                       [v[:, c % 2, kt] for v in xT], kt == 0, kt == KT - 1)
                    return last

                def body(K, c):
                    if is_live(K, c):
                        pe.wait_ge(S("xT_lo"), T("xT_lo", K, c))
                        pe.wait_ge(S("gL_lo"), T("gL_lo", K, c - 1))
                        weighted(bGL, 0, c).then_inc(S("gL_ps"), 1)
                        pe.wait_ge(S("gR_lo"), T("gR_lo", K, c - 1))
                        weighted(bGR, 1, c).then_inc(S("gR_ps"), 1)
                        pe.wait_ge(S("h_lo"), T("h_lo", K, c - 1))
                        pe.matmul(bH[:, 0:D], core.ones[:, :], core.bias[:, bias], start=True, stop=False)
                        for kt in range(KT):
                            last = mm3(pe, bH[:, 0:D], [v[:, c % 2, kt] for v in xT],
                                       [wh[:, 2, kt], wl[:, 2, kt]], False, kt == KT - 1)
                        last.then_inc(S("h_ps"), 1)
                        pe.wait_ge(S("gL_lo"), T("gL_lo", K, c))
                        pe.wait_ge(S("gR_lo"), T("gR_lo", K, c))
                        pe.wait_ge(S("w"), T("w", K, c - 1))
                        for kt in range(KT):
                            last = mm3(pe, bU[:, 0:2 * N], [v[:, c % 2, kt] for v in xT],
                                       [v[:, kt].rearrange("p a b -> p (a b)") for v in g], kt == 0, kt == KT - 1)
                        last.then_inc(S("u_ps"), 1)
                        pe.wait_ge(S(f"loaded{c % U}"), B("loaded", K, c, U, 32))
                        pe.wait_ge(S("mask_l"), T("mask_l", K, c - 1))
                        pe.wait_ge(S("adjT"), T("adjT", K, c - 1))
                        pe.transpose(bA[:, 0:N], adj[:, c % U], core.ident[:, :]).then_inc(S("adjT_ps"), 1)
                    if is_live(K, c + 1):
                        pe.wait_ge(S(f"loaded{(c + 1) % U}"), B("loaded", K, c + 1, U, 32))
                        pe.wait_ge(S("xT_lo"), T("xT_lo", K, c))
                        for kt in range(KT):
                            last = pe.transpose(bT[:, kt * N:(kt + 1) * N], x[:, (c + 1) % U, kt * 128:(kt + 1) * 128],
                                                core.ident[:, :])
                        last.then_inc(S("xT_ps"), 1)
                    if is_live(K, c - 1):
                        pe.wait_ge(S("eT_lo"), T("eT_lo", K, c - 1))
                        pe.wait_ge(S("h_lo"), T("h_lo", K, c - 1))
                        pe.wait_ge(S("t"), T("t", K, c - 2))
                        pe.matmul(bC[:, 0:D + 2], eTs[0][:, :], h[0][:, (c - 1) % 2], start=True, stop=False)
                        pe.matmul(bC[:, 0:D], eTs[0][:, :], h[1][:, (c - 1) % 2, 0:D], start=False, stop=False)
                        pe.matmul(bC[:, 0:D + 2], eTs[1][:, :], h[0][:, (c - 1) % 2], start=False, stop=True)\
                            .then_inc(S("ctx"), 1)
                steps(pe, body, 1)

            @block.scalar
            def _(act):
                def body(K, c):
                    core.next_split(act, core.split_hi, n, K, c)
                    if is_live(K, c - 1):
                        act.wait_ge(S("u"), T("u", K, c - 1))
                        act.activation(e[:, :], u[:, :], ACT.Exp, scale=temper).then_inc(S("exp"), 1)
                    if is_live(K, c - 1):
                        act.wait_ge(S("ea"), T("ea", K, c - 1))
                        act.activation(eTs[0][:, :], ea[:, :], ACT.Copy).then_inc(S("eT_hi"), 1)
                    if is_live(K, c):
                        act.wait_ge(S("gL_ps"), T("gL_ps", K, c))
                        act.activation(g[0][:, :, 0], bGL[:, 0:D].rearrange("p (a b) -> p a b", a=KT), ACT.Copy)\
                            .then_inc(S("gL_hi"), 1)
                    if is_live(K, c - 2):
                        act.wait_ge(S("nq"), T("nq", K, c - 2))
                        act.activation(t[:, c % 2], bC[:, 0:D], ACT.Identity, bias=col(c, NQ), scale=col(c, Q))\
                            .then_inc(S("t"), 1)
                    if is_live(K, c - 3) and closing:
                        act.wait_ge(S("nmr2"), T("nmr2", K, c - 3))
                        act.wait_ge(S(f"stored{(c - 5) % 2}"), B("stored", K, c - 5, 2, 16))
                        act.activation(o[:, (c - 3) % 2], y[:, (c - 3) % 2], ACT.Identity, bias=col(c - 3, NMR2),
                                       scale=col(c - 3, RSTD2)).then_inc(S("o"), 1)
                    if is_live(K, c):
                        act.wait_ge(S("gR_ps"), T("gR_ps", K, c))
                        act.activation(g[0][:, :, 1], bGR[:, 0:D].rearrange("p (a b) -> p a b", a=KT), ACT.Copy)\
                            .then_inc(S("gR_hi"), 1)
                        act.wait_ge(S("h_ps"), T("h_ps", K, c))
                        act.activation(h[0][:, c % 2, 0:D], bH[:, 0:D], ACT.Copy).then_inc(S("h_hi"), 1)
                        act.wait_ge(S("adjT_ps"), T("adjT_ps", K, c))
                        act.activation(adjT[:, c % 2], bA[:, 0:N], ACT.Copy).then_inc(S("adjT"), 1)
                    if is_live(K, c + 1):
                        act.wait_ge(S("xT_ps"), T("xT_ps", K, c + 1))
                        act.activation(xT[0][:, (c + 1) % 2], bT[:, 0:D].rearrange("p (a b) -> p a b", a=KT), ACT.Copy)\
                            .then_inc(S("xT_hi"), 1)
                steps(act, body, 3)

            @block.gpsimd
            def _(pool):
                def body(K, c):
                    core.next_split(pool, core.split_lo, n, K, c)
                    if is_live(K, c - 2):
                        pool.wait_ge(S("agg"), T("agg", K, c - 2))
                        pool.tensor_tensor(col(c, VE), col(c, AG + 1), core.scalar(UNBIASED), ALU.mult).then_inc(S("var1"), 1)
                        pool.wait_ge(S("var1"), T("var1", K, c - 2))
                        pool.tensor_tensor(col(c, SD), col(c, VE), core.scalar(SQRT), ALU.pow).then_inc(S("sigma"), 1)
                    if is_live(K, c - 1):
                        pool.wait_ge(S("eT_hi"), T("eT_hi", K, c - 1))
                        pool.tensor_tensor(eTs[1][:, :], ea[:, :], eTs[0][:, :].bitcast(fp32), ALU.subtract).then_inc(S("eT_lo"), 1)
                    if is_live(K, c - 3) and closing:
                        pool.wait_ge(S("agg2"), T("agg2", K, c - 3))
                        pool.tensor_tensor(col(c - 3, VE2), col(c - 3, AG2 + 1), core.scalar(EPS_OUTER), ALU.add).then_inc(S("veps2"), 1)
                        pool.wait_ge(S("veps2"), T("veps2", K, c - 3))
                        pool.tensor_tensor(col(c - 3, RSTD2), col(c - 3, VE2), core.scalar(INV_SQRT), ALU.pow).then_inc(S("rstd2"), 1)
                    if is_live(K, c):
                        pool.wait_ge(S(f"loaded{c % U}"), B("loaded", K, c, U, 32))
                        pool.wait_ge(S("w"), T("w", K, c - 2))
                        pool.tensor_tensor(mask[:, c % 2, 1], adj[:, c % U], core.upper[:, :], ALU.mult).then_inc(S("mask_r"), 1)
                    if is_live(K, c - 2):
                        pool.wait_ge(S("t"), T("t", K, c - 2))
                        tt = t[:, c % 2]
                        pool.tensor_tensor(tt, tt, core.gain[:, gain], ALU.mult).then_inc(S("gained"), 1)
                        pool.wait_ge(S("gained"), T("gained", K, c - 2))
                        pool.tensor_tensor(tt, tt, core.gain[:, gain + 1], ALU.add).then_inc(S("shifted"), 1)
                steps(pool, body, 3)

            @block.vector
            def _(dve):
                dve.memset(h[0][:, :, D:D + 2].bitcast(fp32), 1.0).then_inc(core.sem("ones_columns"), 1)

                def body(K, c):
                    if is_live(K, c - 1):
                        dve.wait_ge(S("u_ps"), T("u_ps", K, c - 1))
                        dve.wait_ge(S("mask_r"), T("mask_r", K, c - 1))
                        dve.wait_ge(S("mask_l"), T("mask_l", K, c - 1))
                        dve.tensor_tensor(w[:, :, :], bU[:, 0:2 * N].rearrange("p (a b) -> p a b", a=2),
                                          mask[:, (c - 1) % 2], ALU.mult).then_inc(S("w"), 1)
                    if is_live(K, c - 2):
                        dve.wait_ge(S("ctx"), T("ctx", K, c - 2))
                        dve.bn_stats(col(c, ST, 6), bC[:, 0:D]).then_inc(S("bn"), 1)
                    if is_live(K, c - 1):
                        dve.wait_ge(S("w"), T("w", K, c - 1))
                        dve.tensor_tensor(u[:, :], w[:, 0], w[:, 1], ALU.add).then_inc(S("u"), 1)
                    if is_live(K, c - 2):
                        dve.wait_ge(S("bn"), T("bn", K, c - 2))
                        dve.tensor_scalar(col(c, RS), bC[:, D:D + 1], 1e-10, None, ALU.add).then_inc(S("rsum"), 1)
                        dve.bn_aggr(col(c, AG, 2), col(c, ST, 6)).then_inc(S("agg"), 1)
                        dve.wait_ge(S("rsum"), T("rsum", K, c - 2))
                        dve.reciprocal(col(c, RI), col(c, RS)).then_inc(S("rinv"), 1)
                    if is_live(K, c - 3):
                        dve.wait_ge(S("shifted"), T("shifted", K, c - 3))
                        if closing:
                            dve.wait_ge(S(f"residual{(c - 3) % U}"), B("residual", K, c - 3, U, 16))
                            dve.scalar_tensor_tensor(y[:, (c - 3) % 2], t[:, (c - 3) % 2], 0.0, res[:, (c - 3) % U],
                                                     op0=ALU.max, op1=ALU.add).then_inc(S("y"), 1)
                        else:
                            dve.wait_ge(S(f"stored{(c - 5) % 2}"), B("stored", K, c - 5, 2, 16))
                            dve.tensor_scalar(y[:, (c - 3) % 2], t[:, (c - 3) % 2], 0.0, None, ALU.max).then_inc(S("y"), 1)
                    if is_live(K, c - 1):
                        dve.wait_ge(S("exp"), T("exp", K, c - 1))
                        dve.wait_ge(S("adjT"), T("adjT", K, c - 1))
                        dve.wait_ge(S("eT_lo"), T("eT_lo", K, c - 2))
                        dve.tensor_tensor(ea[:, :], e[:, :], adjT[:, (c - 1) % 2], ALU.mult).then_inc(S("ea"), 1)
                    if is_live(K, c - 3) and closing:
                        dve.wait_ge(S("y"), T("y", K, c - 3))
                        dve.bn_stats(col(c - 3, ST2, 6), y[:, (c - 3) % 2]).then_inc(S("bn2"), 1)
                        dve.wait_ge(S("bn2"), T("bn2", K, c - 3))
                    if is_live(K, c - 2):
                        dve.wait_ge(S("sigma"), T("sigma", K, c - 2))
                        dve.wait_ge(S("rinv"), T("rinv", K, c - 2))
                        dve.tensor_scalar(col(c, DEN), col(c, SD), col(c, RI), 1e-3, ALU.mult, ALU.add).then_inc(S("den"), 1)
                    if is_live(K, c - 3) and closing:
                        dve.bn_aggr(col(c - 3, AG2, 2), col(c - 3, ST2, 6)).then_inc(S("agg2"), 1)
                    if is_live(K, c - 2):
                        dve.wait_ge(S("den"), T("den", K, c - 2))
                        dve.reciprocal(col(c, REC), col(c, DEN)).then_inc(S("rec"), 1)
                        dve.wait_ge(S("rec"), T("rec", K, c - 2))
                        dve.tensor_tensor(col(c, Q), col(c, REC), col(c, RI), ALU.mult).then_inc(S("q"), 1)
                        dve.wait_ge(S("q"), T("q", K, c - 2))
                        dve.scalar_tensor_tensor(col(c, NQ), col(c, AG), -1.0, col(c, Q), op0=ALU.mult, op1=ALU.mult)\
                            .then_inc(S("nq"), 1)
                    if is_live(K, c - 3) and closing:
                        dve.wait_ge(S("rstd2"), T("rstd2", K, c - 3))
                        dve.scalar_tensor_tensor(col(c - 3, NMR2), col(c - 3, AG2), -1.0, col(c - 3, RSTD2), op0=ALU.mult,
                                                 op1=ALU.mult).then_inc(S("nmr2"), 1)
                    if is_live(K, c):
                        for i, part, bank in ((0, "gL", bGL), (1, "gR", bGR)):
                            dve.wait_ge(S(part + "_hi"), T(part + "_hi", K, c))
                            dve.tensor_tensor(g[1][:, :, i], bank[:, 0:D].rearrange("p (a b) -> p a b", a=KT),
                                              g[0][:, :, i].bitcast(fp32), ALU.subtract).then_inc(S(part + "_lo"), 1)
                        dve.wait_ge(S("h_hi"), T("h_hi", K, c))
                        dve.tensor_tensor(h[1][:, c % 2, 0:D], bH[:, 0:D], h[0][:, c % 2, 0:D].bitcast(fp32),
                                          ALU.subtract).then_inc(S("h_lo"), 1)
                        dve.wait_ge(S("adjT"), T("adjT", K, c))
                        dve.tensor_tensor(mask[:, c % 2, 0], bA[:, 0:N], core.lowtri[:, :], ALU.mult).then_inc(S("mask_l"), 1)
                    if is_live(K, c + 1):
                        dve.wait_ge(S("xT_hi"), T("xT_hi", K, c + 1))
                        dve.tensor_tensor(xT[1][:, (c + 1) % 2], bT[:, 0:D].rearrange("p (a b) -> p a b", a=KT),
                                          xT[0][:, (c + 1) % 2].bitcast(fp32), ALU.subtract).then_inc(S("xT_lo"), 1)
                steps(dve, body, 3)


def attention(core, n, src, dst):
    nc = core.nc
    ph = Phase(core, n)
    S, T, B = ph.sem, ph.upto, ph.moved
    scale = float(D) ** -0.5
    R = 128 // HEAD
    wh, wl = core.w_hi[:, n % 2], core.w_lo[:, n % 2]
    banks = core.banks
    bQ = bT = banks[4]
    bK = bOT = banks[5]
    bO = banks[6]
    bV = bY = banks[7]
    with ExitStack() as lc:
        sb = lambda name, shape, dt=fp32: lc.enter_context(nc.sbuf_tensor(f"{name}_{n}", shape, dt))
        x = sb("x", [128, U, D])
        adj = sb("adj", [128, U, N])
        xT = [sb(f"xT{i}", [128, 2, KT, N], fp32r) for i in "hl"]
        qT = [sb(f"qT{i}", [128, KT, N], fp32r) for i in "hl"]
        kT = [sb(f"kT{i}", [128, KT, N], fp32r) for i in "hl"]
        vh = sb("vh", [128, U, HEADS, HV], fp32r)
        vl = sb("vl", [128, U, HEADS, HEAD], fp32r)
        a = sb("a", [128, HEADS, N])
        e = sb("e", [128, HEADS, N])
        eTs = [sb(f"eT{i}", [128, HEADS, N], fp32r) for i in "hl"]
        att = sb("att", [128, KT, R, HEAD])
        oT = [sb(f"oT{i}", [128, KT, N], fp32r) for i in "hl"]
        y = sb("y", [128, 2, D])
        o = sb("o", [128, 2, D])
        hs = sb("hs", [128, 2, 6, HEADS])
        MX, MN, NZ, KEEP, RI, RK = range(6)
        sm = sb("sm", [128, 2, 16])
        ST2, AG2, VE2, RSTD2, NMR2 = 0, 6, 8, 9, 10

        def col(c, i, w=1):
            return sm[:, c % 2, i:i + w]

        def per_head(bank, v=HEAD):
            return bank[:, 0:D].rearrange("p (t r d) -> p r t d", t=KT, r=R)

        def grouped(tile):
            return tile.rearrange("p (r t) d -> p r t d", r=R)

        with nc.Block() as block:
            @block.sync
            def _(sp):
                core.load_weights(sp, n + 1)
                io(ph, sp, src, x, adj, None, None, dst, o, "o")

            @block.tensor
            def _(pe):
                for m in range(4):
                    pe.wait_ge(core.sem(f"w_lo{m}"), core.uses(n, m))
                pe.wait_ge(core.sem("ones_columns"), n)

                def transposed(bank, m, c):
                    for mt in range(KT):
                        cols = slice(mt * 128, (mt + 1) * 128)
                        for kt in range(KT):
                            last = mm3(pe, bank[:, cols], [wh[:, m, kt, cols], wl[:, m, kt, cols]],
                                       [v[:, c % 2, kt] for v in xT], kt == 0, kt == KT - 1)
                    return last

                def body(K, c):
                    if is_live(K, c):
                        pe.wait_ge(S("xT_lo"), T("xT_lo", K, c))
                        transposed(bQ, 0, c).then_inc(S("q_ps"), 1)
                        pe.wait_ge(S("oT_lo"), T("oT_lo", K, c - 3))
                        transposed(bK, 1, c).then_inc(S("k_ps"), 1)
                    if is_live(K, c - 2):
                        pe.wait_ge(S("exp"), T("exp", K, c - 2))
                        pe.wait_ge(S("a_parts"), T("a_parts", K, c - 1, per=R))
                        for b in range(KT):
                            for i in range(4):
                                last = pe.transpose(banks[b][:, i * N:(i + 1) * N], e[:, 4 * b + i], core.ident[:, :])
                            last.then_inc(S("eT_ps_parts"), 1)
                    if is_live(K, c):
                        pe.wait_ge(S("y"), T("y", K, c - 3))
                        pe.matmul(bV[:, 0:D], core.ones[:, :], core.bias[:, 3], start=True, stop=False)
                        for kt in range(KT):
                            last = mm3(pe, bV[:, 0:D], [v[:, c % 2, kt] for v in xT],
                                       [wh[:, 2, kt], wl[:, 2, kt]], False, kt == KT - 1)
                        last.then_inc(S("v_ps"), 1)
                    if is_live(K, c - 2):
                        pe.wait_ge(S("v_lo"), T("v_lo", K, c - 2))
                        pe.wait_ge(S("att"), T("att", K, c - 3))
                        for i in range(HEADS):
                            if i % 4 == 0:
                                pe.wait_ge(S("eT_lo_parts"), T("eT_lo_parts", K, c - 2, per=KT, extra=i // 4 - 2))
                            sl = (c - 2) % U
                            out = bO[:, i * HV:(i + 1) * HV]
                            pe.matmul(out, eTs[0][:, i], vh[:, sl, i], start=True, stop=False)
                            pe.matmul(out[:, 0:HEAD], eTs[0][:, i], vl[:, sl, i], start=False, stop=False)
                            last = pe.matmul(out, eTs[1][:, i], vh[:, sl, i], start=False, stop=True)
                        last.then_inc(S("av"), 1)
                    if is_live(K, c + 1):
                        pe.wait_ge(S(f"loaded{(c + 1) % U}"), B("loaded", K, c + 1, U, 32))
                        pe.wait_ge(S("q_lo"), T("q_lo", K, c))
                        for kt in range(KT):
                            last = pe.transpose(bT[:, kt * N:(kt + 1) * N], x[:, (c + 1) % U, kt * 128:(kt + 1) * 128],
                                                core.ident[:, :])
                        last.then_inc(S("xT_ps"), 1)
                    if is_live(K, c):
                        pe.wait_ge(S("q_lo"), T("q_lo", K, c))
                        pe.wait_ge(S("k_lo"), T("k_lo", K, c))
                        pe.wait_ge(S("eT_lo_parts"), T("eT_lo_parts", K, c - 2, per=KT))
                        pe.wait_ge(S("a_parts"), T("a_parts", K, c - 1, per=R))
                        for ct in range(KT):
                            for i, (p, q) in enumerate(((0, 0), (0, 1), (1, 0))):
                                for r in range(R):
                                    rows = slice(r * HEAD, (r + 1) * HEAD)
                                    last = pe.matmul(banks[r][:, ct * N:(ct + 1) * N], qT[p][rows, ct], kT[q][rows, ct],
                                                     start=i == 0, stop=i == 2)
                                    if ct == KT - 1 and i == 2:
                                        last.then_inc(S("scores_parts"), 1)
                    if is_live(K, c - 2):
                        pe.wait_ge(S("att"), T("att", K, c - 2))
                        pe.wait_ge(S("k_lo"), T("k_lo", K, c))
                        for kt in range(KT):
                            last = pe.transpose(bOT[:, kt * N:(kt + 1) * N], att[:, kt].rearrange("p r d -> p (r d)"),
                                                core.ident[:, :])
                        last.then_inc(S("oT_ps"), 1)
                        pe.wait_ge(S("oT_lo"), T("oT_lo", K, c - 2))
                        pe.wait_ge(S("v_lo"), T("v_lo", K, c))
                        pe.matmul(bY[:, 0:D], core.ones[:, :], core.bias[:, 4], start=True, stop=False)
                        for kt in range(KT):
                            last = mm3(pe, bY[:, 0:D], [v[:, kt] for v in oT], [wh[:, 3, kt], wl[:, 3, kt]],
                                       False, kt == KT - 1)
                        last.then_inc(S("y_ps"), 1)
                steps(pe, body, 2)

            def tiles(bank):
                return bank[:, 0:D].rearrange("p (a b) -> p a b", a=KT)

            @block.scalar
            def _(act):
                def body(K, c):
                    core.next_split(act, core.split_hi, n, K, c)
                    if is_live(K, c):
                        act.wait_ge(S("q_ps"), T("q_ps", K, c))
                        act.activation(qT[0][:, :, :], tiles(bQ), ACT.Copy).then_inc(S("q_hi"), 1)
                        act.wait_ge(S("k_ps"), T("k_ps", K, c))
                        act.activation(kT[0][:, :, :], tiles(bK), ACT.Copy).then_inc(S("k_hi"), 1)
                    if is_live(K, c - 2):
                        for b in range(KT):
                            act.wait_ge(S("eT_ps_parts"), T("eT_ps_parts", K, c - 2, per=KT, extra=b - 2))
                            act.activation(eTs[0][:, 4 * b:4 * b + 4], banks[b][:, :].rearrange("p (a b) -> p a b", a=4),
                                           ACT.Copy).then_inc(S("eT_hi_parts"), 1)
                    if is_live(K, c):
                        act.wait_ge(S("v_ps"), T("v_ps", K, c))
                        act.activation(grouped(vh[:, c % U, :, 0:HEAD]), per_head(bV), ACT.Copy).then_inc(S("v_hi"), 1)
                    if is_live(K, c - 3):
                        act.wait_ge(S("nmr2"), T("nmr2", K, c - 3))
                        act.wait_ge(S(f"stored{(c - 5) % 2}"), B("stored", K, c - 5, 2, 16))
                        act.activation(o[:, (c - 3) % 2], y[:, (c - 3) % 2], ACT.Identity, bias=col(c - 3, NMR2),
                                       scale=col(c - 3, RSTD2)).then_inc(S("o"), 1)
                    if is_live(K, c + 1):
                        act.wait_ge(S("xT_ps"), T("xT_ps", K, c + 1))
                        act.activation(xT[0][:, (c + 1) % 2], tiles(bT), ACT.Copy).then_inc(S("xT_hi"), 1)
                    if is_live(K, c - 2):
                        act.wait_ge(S("oT_ps"), T("oT_ps", K, c - 2))
                        act.activation(oT[0][:, :, :], tiles(bOT), ACT.Copy).then_inc(S("oT_hi"), 1)
                    if is_live(K, c - 1):
                        act.wait_ge(S("less_max"), T("less_max", K, c - 1))
                        act.activation(e[:, :, :], e[:, :, :], ACT.Exp).then_inc(S("exp"), 1)
                steps(act, body, 3)

            @block.gpsimd
            def _(pool):
                def body(K, c):
                    core.next_split(pool, core.split_lo, n, K, c)
                    if is_live(K, c - 1):
                        pool.wait_ge(S("max"), T("max", K, c - 1))
                        pool.wait_ge(S("eT_ps_parts"), T("eT_ps_parts", K, c - 2, per=KT))
                        pool.tensor_tensor(e[:, :, :], a[:, :, :],
                                           hs[:, (c - 1) % 2, MX].unsqueeze(2).to_broadcast([128, HEADS, N]),
                                           ALU.subtract).then_inc(S("less_max"), 1)
                    if is_live(K, c - 3):
                        pool.wait_ge(S("agg2"), T("agg2", K, c - 3))
                        pool.tensor_tensor(col(c - 3, VE2), col(c - 3, AG2 + 1), core.scalar(EPS_OUTER), ALU.add).then_inc(S("veps2"), 1)
                        pool.wait_ge(S("veps2"), T("veps2", K, c - 3))
                        pool.tensor_tensor(col(c - 3, RSTD2), col(c - 3, VE2), core.scalar(INV_SQRT), ALU.pow).then_inc(S("rstd2"), 1)
                steps(pool, body, 3)

            @block.vector
            def _(dve):
                dve.memset(vh[:, :, :, HEAD:HV].bitcast(fp32), 1.0).then_inc(core.sem("ones_columns"), 1)

                def minus(lo, whole, hi, event):
                    dve.tensor_tensor(lo, whole, hi, ALU.subtract).then_inc(S(event), 1)

                def body(K, c):
                    if is_live(K, c - 1):
                        dve.wait_ge(S("less_max"), T("less_max", K, c - 2))
                        for r in range(R):
                            dve.wait_ge(S("scores_parts"), T("scores_parts", K, c - 1, per=R, extra=r - 3))
                            dve.scalar_tensor_tensor(a[:, KT * r:KT * (r + 1)], tiles(banks[r]), scale,
                                                     adj[:, (c - 1) % U].unsqueeze(1).to_broadcast([128, KT, N]),
                                                     op0=ALU.mult, op1=ALU.add).then_inc(S("a_parts"), 1)
                    if is_live(K, c - 3):
                        dve.wait_ge(S("y_ps"), T("y_ps", K, c - 3))
                        dve.tensor_tensor(y[:, (c - 3) % 2], bY[:, 0:D], x[:, (c - 3) % U], ALU.add).then_inc(S("y"), 1)
                    if is_live(K, c - 1):
                        dve.wait_ge(S("a_parts"), T("a_parts", K, c - 1, per=R))
                        dve.reduce_max(hs[:, (c - 1) % 2, MX], a[:, :, :], AX.X).then_inc(S("max"), 1)
                    if is_live(K, c - 3):
                        dve.wait_ge(S("y"), T("y", K, c - 3))
                        dve.bn_stats(col(c - 3, ST2, 6), y[:, (c - 3) % 2]).then_inc(S("bn2"), 1)
                    if is_live(K, c - 3):
                        dve.wait_ge(S("bn2"), T("bn2", K, c - 3))
                    if is_live(K, c):
                        dve.wait_ge(S("q_hi"), T("q_hi", K, c))
                        minus(qT[1][:, :, :], tiles(bQ), qT[0][:, :, :].bitcast(fp32), "q_lo")
                    if is_live(K, c - 3):
                        dve.bn_aggr(col(c - 3, AG2, 2), col(c - 3, ST2, 6)).then_inc(S("agg2"), 1)
                    if is_live(K, c):
                        dve.wait_ge(S("k_hi"), T("k_hi", K, c))
                        minus(kT[1][:, :, :], tiles(bK), kT[0][:, :, :].bitcast(fp32), "k_lo")
                    if is_live(K, c - 2):
                        for b in range(KT):
                            dve.wait_ge(S("eT_hi_parts"), T("eT_hi_parts", K, c - 2, per=KT, extra=b - 2))
                            minus(eTs[1][:, 4 * b:4 * b + 4], banks[b][:, :].rearrange("p (a b) -> p a b", a=4),
                                  eTs[0][:, 4 * b:4 * b + 4].bitcast(fp32), "eT_lo_parts")
                    if is_live(K, c - 1):
                        m = hs[:, (c - 1) % 2]
                        dve.tensor_reduce(m[:, MN], a[:, :, :], AX.X, ALU.min).then_inc(S("min"), 1)
                        dve.wait_ge(S("max"), T("max", K, c - 1))
                        dve.tensor_scalar(m[:, NZ], m[:, MX], 0.0, None, ALU.not_equal).then_inc(S("nonzero"), 1)
                        dve.wait_ge(S("min"), T("min", K, c - 1))
                        dve.wait_ge(S("nonzero"), T("nonzero", K, c - 1))
                        dve.scalar_tensor_tensor(m[:, KEEP], m[:, MN], 0.0, m[:, NZ], op0=ALU.not_equal, op1=ALU.max)\
                            .then_inc(S("keep"), 1)
                    if is_live(K, c - 3):
                        dve.wait_ge(S("rstd2"), T("rstd2", K, c - 3))
                        dve.scalar_tensor_tensor(col(c - 3, NMR2), col(c - 3, AG2), -1.0, col(c - 3, RSTD2), op0=ALU.mult,
                                                 op1=ALU.mult).then_inc(S("nmr2"), 1)
                    if is_live(K, c):
                        dve.wait_ge(S("v_hi"), T("v_hi", K, c))
                        minus(grouped(vl[:, c % U]), per_head(bV), grouped(vh[:, c % U, :, 0:HEAD]).bitcast(fp32), "v_lo")
                    if is_live(K, c - 2):
                        dve.wait_ge(S("av"), T("av", K, c - 2))
                        m = hs[:, c % 2]
                        heads = bO[:, 0:HEADS * HV].rearrange("p (h d) -> p h d", h=HEADS)
                        dve.reciprocal(m[:, RI], heads[:, :, HEAD]).then_inc(S("rinv"), 1)
                        dve.wait_ge(S("rinv"), T("rinv", K, c - 2))
                        dve.tensor_tensor(m[:, RK], m[:, RI], m[:, KEEP], ALU.mult).then_inc(S("rkeep"), 1)
                        dve.wait_ge(S("rkeep"), T("rkeep", K, c - 2))
                        dve.tensor_tensor(att[:, :, :, :].rearrange("p t r d -> p r t d"), grouped(heads[:, :, 0:HEAD]),
                                          grouped(m[:, RK].unsqueeze(2).to_broadcast([128, HEADS, HEAD])), ALU.mult)\
                            .then_inc(S("att"), 1)
                    if is_live(K, c + 1):
                        dve.wait_ge(S("xT_hi"), T("xT_hi", K, c + 1))
                        minus(xT[1][:, (c + 1) % 2], tiles(bT), xT[0][:, (c + 1) % 2].bitcast(fp32), "xT_lo")
                    if is_live(K, c - 2):
                        dve.wait_ge(S("oT_hi"), T("oT_hi", K, c - 2))
                        minus(oT[1][:, :, :], tiles(bOT), oT[0][:, :, :].bitcast(fp32), "oT_lo")
                steps(dve, body, 3)


def kernel(**inputs):
    import numpy as _np
    import concourse.bacc as _bacc
    from concourse import mybir as _mybir
    from concourse.bass_utils import run_bass_kernel_spmd as _run

    i = {k: _np.ascontiguousarray(v) for k, v in inputs.items()}
    mats = [i["L0_gnn_W_left"].T, i["L0_gnn_W_self"].T, i["L0_gnn_W_right"].T,
            i["L1_gnn_Wq"].T, i["L1_gnn_Wk"].T, i["L1_gnn_Wv"].T, i["L1_gnn_Wo"].T]
    for l in range(2):
        mats += [i["L2_gnn_W_left"][l], i["L2_gnn_W_right"][l], i["L2_gnn_W_lin"][l].T]
    for l in range(2):
        mats += [i["L3_gnn_Wl"][l].T, i["L3_gnn_Ws"][l].T, i["L3_gnn_Wr"][l].T]
    w = _np.ascontiguousarray(_np.stack(mats).reshape(len(mats), KT, 128, D).transpose(0, 2, 1, 3))
    rows = [i["L0_gnn_b_left"], i["L0_gnn_b_self"], i["L0_gnn_b_right"], i["L1_gnn_bv"], i["L1_gnn_bo"],
            i["L2_gnn_b_lin"][0], i["L2_gnn_b_lin"][1]]
    for l in range(2):
        rows += [i["L3_gnn_bl"][l], i["L3_gnn_bs"][l], i["L3_gnn_br"][l]]
    gains = [i["L0_gnn_gamma"], i["L0_gnn_beta"]]
    for l in range(2):
        gains += [i["L2_gnn_ln_a"][l], i["L2_gnn_ln_b"][l]]
    for l in range(2):
        gains += [i["L3_gnn_ln_w"][l], i["L3_gnn_ln_b"][l]]
    arrays = {"x": i["x"], "adj": i["adj"], "weights": w, "bias_rows": _np.stack(rows), "gain_rows": _np.stack(gains)}

    nc = _bacc.Bacc("TRN2", target_bir_lowering=False, num_devices=1)
    args = [nc.dram_tensor(k, a.shape, _mybir.dt.from_np(a.dtype), kind="ExternalInput").ap() for k, a in arrays.items()]
    out = nc.dram_tensor("out", (G, N, D), _mybir.dt.float32, kind="ExternalOutput").ap()
    scratch = [nc.dram_tensor(f"scratch{k}", (G, N, D), _mybir.dt.float32, kind="Internal").ap() for k in range(5)]
    program(nc, *args, out, scratch)
    r = _run(nc, [arrays], core_ids=[0])
    return r.results[0]["out"]
```

```python
import concourse.bass as bass
from concourse import mybir
from contextlib import ExitStack

G, N, D = 64, 128, 384
KT = D // 128
U = 4
HEADS, HEAD = 12, 32
HV = HEAD + 1
NB = 13
LO_ROW = 32
NG = 11

fp32 = mybir.dt.float32
fp32r = mybir.dt.float32r
ALU = mybir.AluOpType
ACT = mybir.ActivationFunctionType
AX = mybir.AxisListType

SCALARS = [-0.5, 0.5, 1e-12, 1e-5, float(D) / (D - 1)]
INV_SQRT, SQRT, EPS_INNER, EPS_OUTER, UNBIASED = range(5)


LAST = (G - U) // 2


def is_live(K, c):
    return not isinstance(K, int) or 0 <= 2 * K + c < G


def steps(eng, body, tail, head=1):
    for c in range(-head, 2 * U):
        body(0, c)
    with eng.Fori(U, LAST - U // 2 + 1, U // 2) as K:
        for c in range(U):
            body(K, c)
    for c in range(U + tail):
        body(LAST, c)


def program(nc, x_in, adj_in, w_in, bias_in, gain_in, out, scratch):
    ctx = ExitStack()
    with ctx:
        core = Core(nc, ctx, x_in, adj_in, w_in, bias_in, gain_in)
        digcn(core, 0, x_in, x_in, scratch[0], bias=0, gain=0, closing=True)
        attention(core, 1, scratch[0], scratch[1])
        exp_gnn(core, 2, scratch[1], None, scratch[2], gain=2, bias=5)
        exp_gnn(core, 3, scratch[2], scratch[1], scratch[3], gain=4, bias=6)
        digcn(core, 4, scratch[3], None, scratch[4], bias=7, gain=6, closing=False)
        digcn(core, 5, scratch[4], scratch[3], out, bias=10, gain=8, closing=True)


WEIGHTS = [(0, 3), (3, 4), (7, 3), (10, 3), (13, 3), (16, 3)]


class Core:

    def __init__(self, nc, ctx, x_in, adj_in, w_in, bias_in, gain_in):
        self.nc, self.ctx, self.sems, self.phases_with = nc, ctx, {}, {}
        self.adj_in, self.w_in, self.bias_in, self.gain_in = adj_in, w_in, bias_in, gain_in
        self.ident = self.sb("ident", [128, 128])
        self.upper = self.sb("upper", [128, 128])
        self.lower = self.sb("lower", [128, 128])
        self.lowtri = self.sb("lowtri", [128, 128])
        self.ones = self.sb("ones", [128, 128], fp32r)
        self.scalars = self.sb("scalars", [128, len(SCALARS)])
        self.bias = self.sb("bias", [128, NB, D], fp32r)
        self.gain = self.sb("gain", [128, NG, D])
        self.w_raw = self.sb("w_raw", [128, 4, KT, D])
        self.w_hi = self.sb("w_hi", [128, 2, 4, KT, D], fp32r)
        self.w_lo = self.sb("w_lo", [128, 2, 4, KT, D], fp32r)
        self.banks = [ctx.enter_context(nc.psum_tensor(f"bank{i}", [128, 512], fp32)) for i in range(8)]

    def scalar(self, k):
        return self.scalars[:, k:k + 1]

    def sb(self, name, shape, dt=fp32):
        return self.ctx.enter_context(self.nc.sbuf_tensor(name, shape, dt))

    def sem(self, name):
        if name not in self.sems:
            self.sems[name] = self.ctx.enter_context(self.nc.semaphore(name))
        return self.sems[name]

    def load_weights(self, sp, n):
        first, count = WEIGHTS[n]
        for m in range(count):
            if n:
                before = [p for p in range(n) if m < WEIGHTS[p][1]]
                if before:
                    sp.wait_ge(self.sem(f"w_lo{m}"), len(before))
            sp.dma_start(self.w_raw[:, m], self.w_in[first + m]).then_inc(self.sem(f"w_loaded{m}"), 16)

    def uses(self, n, m):
        return sum(m < WEIGHTS[p][1] for p in range(n + 1))

    def split_hi(self, act, n, m):
        act.wait_ge(self.sem(f"w_loaded{m}"), 16 * self.uses(n, m))
        act.activation(self.w_hi[:, n % 2, m], self.w_raw[:, m], ACT.Copy).then_inc(self.sem(f"w_hi{m}"), 1)

    def split_lo(self, pool, n, m):
        pool.wait_ge(self.sem(f"w_hi{m}"), self.uses(n, m))
        pool.tensor_tensor(self.w_lo[:, n % 2, m], self.w_raw[:, m],
                           self.w_hi[:, n % 2, m].bitcast(fp32), ALU.subtract).then_inc(self.sem(f"w_lo{m}"), 1)

    def next_split(self, eng, split, n, K, c):
        if isinstance(K, int) and K == LAST and n + 1 < len(WEIGHTS) and 0 <= c < WEIGHTS[n + 1][1]:
            split(eng, n + 1, c)


FIRST, OTHERS = slice(0, 3), slice(3, NB)


def bias_hi(core, act, raw, rows):
    act.wait_ge(core.sem("bias_clear"), 1 if rows is FIRST else 2)
    for p in (0, LO_ROW):
        act.activation(core.bias[p:p + 1, rows], raw[p:p + 1, rows], ACT.Copy).then_inc(core.sem("bias_hi"), 1)


def bias_lo(core, dve, raw, rows):
    dve.wait_ge(core.sem("bias_hi"), 2 if rows is FIRST else 4)
    p = slice(LO_ROW, LO_ROW + 1)
    dve.tensor_tensor(core.bias[p, rows], raw[p, rows], core.bias[p, rows].bitcast(fp32), ALU.subtract)\
        .then_inc(core.sem("bias_ready"), 1)


def setup_sync(core, sp, raw):
    for p in (0, LO_ROW):
        sp.dma_start(raw[p:p + 1], core.bias_in.unsqueeze(0)).then_inc(core.sem("bias_loaded"), 16)
    core.load_weights(sp, 0)


def setup_gpsimd(core, pool):
    s = core.sem
    for t in (core.ident, core.upper, core.lower, core.lowtri):
        pool.memset(t[:, :], 0.0 if t is core.ident else 1.0).then_inc(s("consts"), 1)
    pool.wait_ge(s("consts"), 4)
    for t, op, fill in ((core.ident, ALU.not_equal, 1.0), (core.lowtri, ALU.is_ge, 0.0), (core.lower, ALU.is_gt, 0.0)):
        pool.affine_select(out=t[:, :], in_=t[:, :], compare_op=op, fill=fill, base=0,
                           pattern=[[-1, 128]], channel_multiplier=1).then_inc(s("consts"), 1)
    pool.affine_select(out=core.upper[:, :], in_=core.upper[:, :], compare_op=ALU.is_gt, fill=0.0, base=0,
                       pattern=[[1, 128]], channel_multiplier=-1).then_inc(s("consts"), 1)
    for k, value in enumerate(SCALARS):
        pool.memset(core.scalars[:, k:k + 1], value).then_inc(s("consts"), 1)
    pool.memset(core.ones[:, :].bitcast(fp32), 1.0).then_inc(s("ones"), 1)


def setup_scalar(core, act, raw):
    act.wait_ge(core.sem("bias_loaded"), 2 * 16)
    bias_hi(core, act, raw, FIRST)
    for m in range(WEIGHTS[0][1]):
        core.split_hi(act, 0, m)


def setup_vector(core, dve, raw):
    for rows in (FIRST, OTHERS):
        dve.memset(core.bias[:, rows].bitcast(fp32), 0.0).then_inc(core.sem("bias_clear"), 1)
    bias_lo(core, dve, raw, FIRST)
    for m in range(WEIGHTS[0][1]):
        core.split_lo(dve, 0, m)
    dve.wait_ge(core.sem("consts"), 8 + len(SCALARS))


class Phase:

    def __init__(self, core, n):
        self.core, self.n, self.used = core, n, set()

    def base(self, name):
        if name not in self.used:
            self.used.add(name)
            self.core.phases_with[name] = self.core.phases_with.get(name, 0) + 1
        return G * (self.core.phases_with[name] - 1)

    def sem(self, name):
        self.base(name)
        return self.core.sem(name)

    def upto(self, name, K, c, per=1, extra=0):
        if isinstance(K, int):
            c = min(c, G - 1 - 2 * K)
        count = K * (2 * per) + (self.base(name) + c + 1) * per + extra
        return max(count, 0) if isinstance(K, int) else count

    def pairs(self, name, K, c, per=1, extra=0):
        if isinstance(K, int):
            c = min(c, G - 1 - 2 * K)
        count = K * per + (self.base(name) // 2 + c // 2 + 1) * per + extra
        return max(count, 0) if isinstance(K, int) else count

    def moved(self, name, K, c, slots, per):
        count = K * (2 * per // slots) + (self.base(f"{name}{c % slots}") // slots + c // slots + 1) * per
        return max(count, 0) if isinstance(K, int) else count


def mm3(pe, out, lhs, rhs, first, last):
    pe.matmul(out, lhs[0], rhs[0], start=first, stop=False)
    pe.matmul(out, lhs[0], rhs[1], start=False, stop=False)
    return pe.matmul(out, lhs[1], rhs[0], start=False, stop=last)


def tile_of(dram, K, c):
    if isinstance(K, int):
        return dram[2 * K + c]
    return dram[bass.ds(K * 2 + c, 1)].rearrange("a p d -> (a p) d")


def digcn(core, n, x_src, res_src, dst, bias, gain, closing):
    nc = core.nc
    ph = Phase(core, n)
    S, T, B = ph.sem, ph.upto, ph.moved
    temper = float(D) ** -0.5
    wh, wl = core.w_hi[:, n % 2], core.w_lo[:, n % 2]
    bT, bS, bL, bR, bH, bE, bC = (core.banks[i] for i in range(7))
    with ExitStack() as lc:
        sb = lambda name, shape, dt=fp32: lc.enter_context(nc.sbuf_tensor(f"{name}_{n}", shape, dt))
        x = sb("x", [128, U, D])
        res = sb("res", [128, U, D]) if closing else None
        adj = sb("adj", [128, U, N])
        xT = [sb(f"xT{i}", [128, 2, KT, N], fp32r) for i in "hl"]
        xT32 = sb("xT32", [128, 2, KT, N])
        hL = [sb(f"hL{i}", [128, 2, D], fp32r) for i in "hl"]
        hR = [sb(f"hR{i}", [128, 2, D], fp32r) for i in "hl"]
        selfp = sb("selfp", [128, 2, D])
        e = sb("e", [128, N])
        delta = sb("delta", [128, 2, N])
        dscr = sb("dscr", [128, N])
        eT = sb("eT", [128, 2, N])
        eTs = [sb(f"eT{i}", [128, 2, N], fp32r) for i in "hl"]
        z = sb("z", [128, 2, D])
        t = sb("t", [128, 2, D])
        y = sb("y", [128, 2, D])
        bias_raw = sb("bias_raw", [LO_ROW + 1, NB, D]) if n == 0 else None
        o = sb("o", [128, 2, D])
        sm = sb("sm", [128, 2, 32])
        MX, NM, ES, DS, RS, RI, DG = range(7)
        ST, AG, VE, RSTD, NMR = 8, 14, 16, 17, 18
        ST2, AG2, VE2, RSTD2, NMR2 = 20, 26, 28, 29, 30

        def col(c, i, w=1):
            return sm[:, c % 2, i:i + w]

        with nc.Block() as block:
            @block.sync
            def _(sp):
                if n == 0:
                    setup_sync(core, sp, bias_raw)
                result, event = (o, "o") if closing else (y, "y")

                def body(K, c):
                    if is_live(K, c - 4):
                        sp.wait_ge(S(event), T(event, K, c - 4))
                        sp.dma_start(tile_of(dst, K, c - 4), result[:, c % 2]).then_inc(S(f"stored{c % 2}"), 16)
                    if is_live(K, c + 3):
                        sp.wait_ge(S("xT_ps"), T("xT_ps", K, c + 3 - U))
                        sl = (c + 3) % U
                        sp.dma_start(x[:, sl], tile_of(x_src, K, c + 3)).then_inc(S(f"loaded{sl}"), 16)
                    if is_live(K, c + 2):
                        sp.wait_ge(S("delta"), T("delta", K, c + 2 - U))
                        sl = (c + 2) % U
                        sp.dma_start(adj[:, sl], tile_of(core.adj_in, K, c + 2)).then_inc(S(f"adjacency{sl}"), 16)
                    if isinstance(K, int) and K == 0 and c == 0:
                        if n == 0:
                            sp.dma_start(core.gain[:, :, :], core.gain_in.unsqueeze(0).to_broadcast([128, NG, D]))\
                                .then_inc(core.sem("gain_loaded"), 16)
                        if n + 1 < len(WEIGHTS):
                            core.load_weights(sp, n + 1)
                    if closing and is_live(K, c + 1):
                        sp.wait_ge(S("y"), T("y", K, c + 1 - U))
                        sl = (c + 1) % U
                        sp.dma_start(res[:, sl], tile_of(res_src, K, c + 1)).then_inc(S(f"residual{sl}"), 16)
                steps(sp, body, 4, head=3)
                for i in range(2):
                    sp.wait_ge(S(f"stored{i}"), T(f"stored{i}", LAST, U - 1) * 8)

            @block.tensor
            def _(pe):
                pe.wait_ge(core.sem("consts"), 8 + len(SCALARS))

                def project(K, bank, m, c):
                    if isinstance(K, int) and K == 0 and c == 0:
                        pe.wait_ge(core.sem(f"w_lo{m}"), core.uses(n, m))
                        pe.wait_ge(core.sem("bias_ready"), 1)
                        pe.wait_ge(core.sem("ones"), 1)
                    pe.matmul(bank[:, 0:D], core.ones[:, :], core.bias[:, bias + m], start=True, stop=False)
                    for kt in range(KT):
                        last = mm3(pe, bank[:, 0:D], [v[:, c % 2, kt] for v in xT],
                                   [wh[:, m, kt], wl[:, m, kt]], False, kt == KT - 1)
                    return last

                def body(K, c):
                    if is_live(K, c):
                        pe.wait_ge(S("xT32"), T("xT32", K, c))
                        pe.wait_ge(S("exp"), T("exp", K, c - 1))
                        for kt in range(KT):
                            last = pe.matmul(bS[:, 0:N], xT32[:, c % 2, kt], xT32[:, c % 2, kt],
                                             start=kt == 0, stop=kt == KT - 1)
                        last.then_inc(S("scores"), 1)
                        pe.wait_ge(S("xT_lo"), T("xT_lo", K, c))
                        pe.wait_ge(S("hL_lo"), T("hL_lo", K, c - 1))
                        project(K, bL, 0, c).then_inc(S("hL_ps"), 1)
                    if is_live(K, c - 1):
                        pe.wait_ge(S("delta"), T("delta", K, c - 1))
                        pe.wait_ge(S("eT"), T("eT", K, c - 2))
                        pe.transpose(bE[:, 0:N], delta[:, (c - 1) % 2], core.ident[:, :]).then_inc(S("eT_ps"), 1)
                    if is_live(K, c):
                        pe.wait_ge(S("hR_lo"), T("hR_lo", K, c - 1))
                        project(K, bR, 2, c).then_inc(S("hR_ps"), 1)
                    if is_live(K, c + 1):
                        pe.wait_ge(S(f"loaded{(c + 1) % U}"), B("loaded", K, c + 1, U, 16))
                        pe.wait_ge(S("xT_lo"), T("xT_lo", K, c))
                        pe.wait_ge(S("xT32"), T("xT32", K, c))
                        for kt in range(KT):
                            last = pe.transpose(bT[:, kt * N:(kt + 1) * N], x[:, (c + 1) % U, kt * 128:(kt + 1) * 128],
                                                core.ident[:, :])
                        last.then_inc(S("xT_ps"), 1)
                    if is_live(K, c):
                        pe.wait_ge(S("self"), T("self", K, c - 1))
                        project(K, bH, 1, c).then_inc(S("self_ps"), 1)
                    if is_live(K, c - 1):
                        pe.wait_ge(S("eT_lo"), T("eT_lo", K, c - 1))
                        pe.wait_ge(S("hL_lo"), T("hL_lo", K, c - 1))
                        pe.wait_ge(S("hR_lo"), T("hR_lo", K, c - 1))
                        pe.wait_ge(S("z"), T("z", K, c - 2))
                        mm3(pe, bC[:, 0:D], [v[:, 0] for v in eTs], [v[:, (c - 1) % 2] for v in hL], True, False)
                        mm3(pe, bC[:, 0:D], [v[:, 1] for v in eTs], [v[:, (c - 1) % 2] for v in hR], False, True)\
                            .then_inc(S("ctx"), 1)
                steps(pe, body, 1)

            @block.scalar
            def _(act):
                if n == 0:
                    setup_scalar(core, act, bias_raw)

                def body(K, c):
                    core.next_split(act, core.split_hi, n, K, c)
                    if n == 0 and isinstance(K, int) and K == LAST and c == U + 1:
                        bias_hi(core, act, bias_raw, OTHERS)
                    if is_live(K, c):
                        act.wait_ge(S("negmax"), T("negmax", K, c))
                        act.activation(e[:, :], bS[:, 0:N], ACT.Exp, bias=col(c, NM), scale=temper,
                                       accum_out=col(c, ES)).then_inc(S("exp"), 1)
                        act.wait_ge(S("hL_ps"), T("hL_ps", K, c))
                        act.activation(hL[0][:, c % 2], bL[:, 0:D], ACT.Copy).then_inc(S("hL_hi"), 1)
                    if is_live(K, c - 2):
                        act.wait_ge(S("nmr"), T("nmr", K, c - 2))
                        act.activation(t[:, (c - 2) % 2], z[:, (c - 2) % 2], ACT.Identity, bias=col(c - 2, NMR),
                                       scale=col(c - 2, RSTD)).then_inc(S("t"), 1)
                    if is_live(K, c - 1):
                        act.wait_ge(S("eT"), T("eT", K, c - 1))
                        act.activation(eTs[0][:, :, :], eT[:, :, :], ACT.Copy).then_inc(S("eT_hi"), 1)
                    if is_live(K, c):
                        act.wait_ge(S("hR_ps"), T("hR_ps", K, c))
                        act.activation(hR[0][:, c % 2], bR[:, 0:D], ACT.Copy).then_inc(S("hR_hi"), 1)
                    if is_live(K, c + 1):
                        act.wait_ge(S("xT_ps"), T("xT_ps", K, c + 1))
                        act.activation(xT[0][:, (c + 1) % 2], bT[:, 0:D], ACT.Copy).then_inc(S("xT_hi"), 1)
                        act.activation(xT32[:, (c + 1) % 2], bT[:, 0:D], ACT.Copy).then_inc(S("xT32"), 1)
                    if is_live(K, c - 3) and closing:
                        act.wait_ge(S("nmr2"), T("nmr2", K, c - 3))
                        act.wait_ge(S(f"stored{(c - 5) % 2}"), B("stored", K, c - 5, 2, 16))
                        act.activation(o[:, (c - 3) % 2], y[:, (c - 3) % 2], ACT.Identity, bias=col(c - 3, NMR2),
                                       scale=col(c - 3, RSTD2)).then_inc(S("o"), 1)
                    if is_live(K, c):
                        act.wait_ge(S("self_ps"), T("self_ps", K, c))
                        act.wait_ge(S("diag"), T("diag", K, c))
                        act.wait_ge(S("z"), T("z", K, c - 2))
                        act.activation(selfp[:, c % 2], bH[:, 0:D], ACT.Copy, scale=col(c, DG)).then_inc(S("self"), 1)
                steps(act, body, 3)

            @block.gpsimd
            def _(pool):
                if n == 0:
                    setup_gpsimd(core, pool)

                def body(K, c):
                    core.next_split(pool, core.split_lo, n, K, c)
                    if is_live(K, c - 2):
                        pool.wait_ge(S("agg"), T("agg", K, c - 2))
                        pool.tensor_tensor(col(c - 2, VE), col(c - 2, AG + 1), core.scalar(EPS_INNER), ALU.add).then_inc(S("veps"), 1)
                        pool.wait_ge(S("veps"), T("veps", K, c - 2))
                        pool.tensor_tensor(col(c - 2, RSTD), col(c - 2, VE), core.scalar(INV_SQRT), ALU.pow).then_inc(S("rstd"), 1)
                    if is_live(K, c - 3) and closing:
                        pool.wait_ge(S("agg2"), T("agg2", K, c - 3))
                        pool.tensor_tensor(col(c - 3, VE2), col(c - 3, AG2 + 1), core.scalar(EPS_OUTER), ALU.add).then_inc(S("veps2"), 1)
                        pool.wait_ge(S("veps2"), T("veps2", K, c - 3))
                        pool.tensor_tensor(col(c - 3, RSTD2), col(c - 3, VE2), core.scalar(INV_SQRT), ALU.pow).then_inc(S("rstd2"), 1)
                    if is_live(K, c - 1):
                        pool.wait_ge(S("eT_hi"), T("eT_hi", K, c - 1))
                        pool.tensor_tensor(eTs[1][:, :, :], eT[:, :, :], eTs[0][:, :, :].bitcast(fp32),
                                           ALU.subtract).then_inc(S("eT_lo"), 1)
                    if is_live(K, c - 2):
                        pool.wait_ge(S("t"), T("t", K, c - 2))
                        pool.wait_ge(core.sem("gain_loaded"), 16)
                        tt = t[:, (c - 2) % 2]
                        pool.tensor_tensor(tt, tt, core.gain[:, gain], ALU.mult).then_inc(S("gained"), 1)
                        pool.wait_ge(S("gained"), T("gained", K, c - 2))
                        pool.tensor_tensor(tt, tt, core.gain[:, gain + 1], ALU.add).then_inc(S("shifted"), 1)
                steps(pool, body, 3)

            @block.vector
            def _(dve):
                if n == 0:
                    setup_vector(core, dve, bias_raw)

                def body(K, c):
                    if n == 0 and isinstance(K, int) and K == LAST and c == U + 2:
                        bias_lo(core, dve, bias_raw, OTHERS)
                    if is_live(K, c - 2):
                        dve.wait_ge(S("ctx"), T("ctx", K, c - 2))
                        dve.wait_ge(S("self"), T("self", K, c - 2))
                        dve.scalar_tensor_tensor(z[:, (c - 2) % 2], bC[:, 0:D], col(c - 2, RI), selfp[:, (c - 2) % 2],
                                                 op0=ALU.mult, op1=ALU.add).then_inc(S("z"), 1)
                    if is_live(K, c):
                        dve.wait_ge(S("scores"), T("scores", K, c))
                        dve.reduce_max(col(c, MX), bS[:, 0:N], AX.X).then_inc(S("max"), 1)
                    if is_live(K, c - 2):
                        dve.wait_ge(S("z"), T("z", K, c - 2))
                        dve.bn_stats(col(c - 2, ST, 6), z[:, (c - 2) % 2]).then_inc(S("bn"), 1)
                    if is_live(K, c - 2):
                        dve.wait_ge(S("bn"), T("bn", K, c - 2))
                    if is_live(K, c):
                        dve.wait_ge(S("max"), T("max", K, c))
                        dve.tensor_scalar(col(c, NM), col(c, MX), -temper, None, ALU.mult).then_inc(S("negmax"), 1)
                    if is_live(K, c - 2):
                        dve.bn_aggr(col(c - 2, AG, 2), col(c - 2, ST, 6)).then_inc(S("agg"), 1)
                    if is_live(K, c - 3):
                        dve.wait_ge(S("shifted"), T("shifted", K, c - 3))
                        if closing:
                            dve.wait_ge(S(f"residual{(c - 3) % U}"), B("residual", K, c - 3, U, 16))
                            dve.scalar_tensor_tensor(y[:, (c - 3) % 2], t[:, (c - 3) % 2], 0.0, res[:, (c - 3) % U],
                                                     op0=ALU.max, op1=ALU.add).then_inc(S("y"), 1)
                        else:
                            dve.wait_ge(S(f"stored{(c - 5) % 2}"), B("stored", K, c - 5, 2, 16))
                            dve.tensor_scalar(y[:, (c - 3) % 2], t[:, (c - 3) % 2], 0.0, None, ALU.max).then_inc(S("y"), 1)
                    if is_live(K, c):
                        dve.wait_ge(S("exp"), T("exp", K, c))
                        dve.wait_ge(S(f"adjacency{c % U}"), B("adjacency", K, c, U, 16))
                        dve.wait_ge(S("eT_ps"), T("eT_ps", K, c - 2))
                        dve.scalar_tensor_tensor(delta[:, c % 2], e[:, :], 1.0, adj[:, c % U], op0=ALU.mult,
                                                 op1=ALU.mult, accum_out=col(c, DS)).then_inc(S("delta"), 1)
                    if is_live(K, c - 3) and closing:
                        dve.wait_ge(S("y"), T("y", K, c - 3))
                        dve.bn_stats(col(c - 3, ST2, 6), y[:, (c - 3) % 2]).then_inc(S("bn2"), 1)
                    if is_live(K, c - 3) and closing:
                        dve.wait_ge(S("bn2"), T("bn2", K, c - 3))
                    if is_live(K, c):
                        dve.wait_ge(S("delta"), T("delta", K, c))
                        dve.scalar_tensor_tensor(col(c, RS), col(c, ES), 1e-10, col(c, DS), op0=ALU.mult,
                                                 op1=ALU.add).then_inc(S("rsum"), 1)
                    if is_live(K, c - 3) and closing:
                        dve.bn_aggr(col(c - 3, AG2, 2), col(c - 3, ST2, 6)).then_inc(S("agg2"), 1)
                    if is_live(K, c):
                        dve.wait_ge(S("rsum"), T("rsum", K, c))
                        dve.reciprocal(col(c, RI), col(c, RS)).then_inc(S("rinv"), 1)
                    if is_live(K, c - 2):
                        dve.wait_ge(S("rstd"), T("rstd", K, c - 2))
                        dve.scalar_tensor_tensor(col(c - 2, NMR), col(c - 2, AG), -1.0, col(c - 2, RSTD), op0=ALU.mult,
                                                 op1=ALU.mult).then_inc(S("nmr"), 1)
                    if is_live(K, c):
                        dve.wait_ge(S("hL_hi"), T("hL_hi", K, c))
                        dve.tensor_tensor(hL[1][:, c % 2], bL[:, 0:D], hL[0][:, c % 2].bitcast(fp32),
                                          ALU.subtract).then_inc(S("hL_lo"), 1)
                    if is_live(K, c - 1):
                        dve.wait_ge(S("eT_ps"), T("eT_ps", K, c - 1))
                        dve.wait_ge(S("eT_lo"), T("eT_lo", K, c - 2))
                        dve.tensor_tensor(eT[:, 0], bE[:, 0:N], core.lower[:, :], ALU.mult).then_inc(S("eT_u"), 1)
                        dve.tensor_tensor(eT[:, 1], bE[:, 0:N], core.upper[:, :], ALU.mult).then_inc(S("eT"), 1)
                    if is_live(K, c):
                        dve.wait_ge(S("rinv"), T("rinv", K, c))
                        dve.tensor_tensor_reduce(out=dscr[:, :], in0=delta[:, c % 2], in1=core.ident[:, :],
                                                 scale=col(c, RI), scalar=0.0, op0=ALU.mult, op1=ALU.add,
                                                 accum_out=col(c, DG)).then_inc(S("diag"), 1)
                    if is_live(K, c - 3) and closing:
                        dve.wait_ge(S("rstd2"), T("rstd2", K, c - 3))
                        dve.scalar_tensor_tensor(col(c - 3, NMR2), col(c - 3, AG2), -1.0, col(c - 3, RSTD2), op0=ALU.mult,
                                                 op1=ALU.mult).then_inc(S("nmr2"), 1)
                    if is_live(K, c):
                        dve.wait_ge(S("hR_hi"), T("hR_hi", K, c))
                        dve.tensor_tensor(hR[1][:, c % 2], bR[:, 0:D], hR[0][:, c % 2].bitcast(fp32),
                                          ALU.subtract).then_inc(S("hR_lo"), 1)
                    if is_live(K, c + 1):
                        dve.wait_ge(S("xT32"), T("xT32", K, c + 1))
                        dve.tensor_tensor(xT[1][:, (c + 1) % 2], bT[:, 0:D], xT[0][:, (c + 1) % 2].bitcast(fp32),
                                          ALU.subtract).then_inc(S("xT_lo"), 1)

                steps(dve, body, 3)


def exp_gnn(core, n, x_src, res_src, dst, gain, bias):
    nc = core.nc
    closing = res_src is not None
    ph = Phase(core, n)
    S, T, P2, B = ph.sem, ph.upto, ph.pairs, ph.moved
    temper = float(D) ** -0.5
    wh, wl = core.w_hi[:, n % 2], core.w_lo[:, n % 2]
    bG, (bT, bH, bU, bA, bC) = core.banks[0:3], core.banks[3:8]
    GP = 2 * KT
    with ExitStack() as lc:
        sb = lambda name, shape, dt=fp32: lc.enter_context(nc.sbuf_tensor(f"{name}_{n}", shape, dt))
        x = sb("x", [128, U, D])
        res = sb("res", [128, U, D]) if closing else None
        adj = sb("adj", [128, U, N])
        xT = [sb(f"xT{i}", [128, 2, KT, 2, N], fp32r) for i in "hl"]
        g = [sb(f"g{i}", [128, GP, 2, N], fp32r) for i in "hl"]
        h = [sb(f"h{i}", [128, 2, D + 2], fp32r) for i in "hl"]
        adjT = sb("adjT", [128, 2, N])
        mask = sb("mask", [128, 2, 2, N])
        w = sb("w", [128, 2, N])
        u = sb("u", [128, N])
        e = sb("e", [128, N])
        ea = sb("ea", [128, N])
        eTs = [sb(f"eT{i}", [128, 2, N], fp32r) for i in "hl"]
        t = sb("t", [128, 2, D])
        y = sb("y", [128, 2, D])
        o = sb("o", [128, 2, D])
        sm = sb("sm", [128, 2, 32])
        ST, AG, RS, VE, SD, DEN, Q, NQ = 0, 6, 8, 9, 10, 11, 12, 13
        ST2, AG2, VE2, RSTD2, NMR2 = 16, 22, 24, 25, 26

        def col(c, i, w=1):
            return sm[:, c % 2, i:i + w]

        def xT_of(c):
            return [v[:, c // 2 % 2, :, c % 2] for v in xT]

        def tiles(bank):
            return bank[:, 0:D].rearrange("p (a b) -> p a b", a=KT)

        def chunk(v, j):
            return v[:, 2 * j:2 * j + 2].rearrange("p a b c -> p (a b c)")

        with nc.Block() as block:
            @block.sync
            def _(sp):
                if n + 1 < len(WEIGHTS):
                    core.load_weights(sp, n + 1)
                result, event = (o, "o") if closing else (y, "y")

                def body(K, c):
                    if is_live(K, c - 4):
                        sp.wait_ge(S(event), T(event, K, c - 4))
                        sp.dma_start(tile_of(dst, K, c - 4), result[:, c % 2]).then_inc(S(f"stored{c % 2}"), 16)
                    if is_live(K, c + 4):
                        sp.wait_ge(S("xT_ps"), T("xT_ps", K, c + 4 - U))
                        sl = (c + 4) % U
                        sp.dma_start(x[:, sl], tile_of(x_src, K, c + 4)).then_inc(S(f"loaded{sl}"), 16)
                    if is_live(K, c + 3):
                        sp.wait_ge(S("mask_r"), T("mask_r", K, c + 3 - U))
                        sp.wait_ge(S("adjT_ps"), T("adjT_ps", K, c + 3 - U))
                        sl = (c + 3) % U
                        sp.dma_start(adj[:, sl], tile_of(core.adj_in, K, c + 3)).then_inc(S(f"adjacency{sl}"), 16)
                    if closing and is_live(K, c + 1):
                        sp.wait_ge(S("y"), T("y", K, c + 1 - U))
                        sl = (c + 1) % U
                        sp.dma_start(res[:, sl], tile_of(res_src, K, c + 1)).then_inc(S(f"residual{sl}"), 16)
                steps(sp, body, 4, head=4)
                for i in range(2):
                    sp.wait_ge(S(f"stored{i}"), T(f"stored{i}", LAST, U - 1) * 8)

            @block.tensor
            def _(pe):
                for m in range(3):
                    pe.wait_ge(core.sem(f"w_lo{m}"), core.uses(n, m))
                pe.wait_ge(core.sem("ones_columns"), n)

                def pair_product(K, c, j):
                    pe.wait_ge(S("g_lo"), P2("g_lo", K, c - 2, per=KT, extra=j - 2))
                    for k in (2 * j, 2 * j + 1):
                        cols = slice(k % KT * 128, (k % KT + 1) * 128)
                        for kt in range(KT):
                            last = mm3(pe, bG[j][:, k % 2 * 2 * N:(k % 2 + 1) * 2 * N],
                                       [wh[:, k // KT, kt, cols], wl[:, k // KT, kt, cols]],
                                       [v[:, c // 2 % 2, kt].rearrange("p a b -> p (a b)") for v in xT],
                                       kt == 0, kt == KT - 1)
                    last.then_inc(S("g_ps"), 1)

                def body(K, c):
                    if c % 2 == 0 and is_live(K, c):
                        pe.wait_ge(S("xT_lo"), T("xT_lo", K, c + 1))
                        pair_product(K, c, 0)
                    if is_live(K, c - 2):
                        pe.wait_ge(S("eT_lo"), T("eT_lo", K, c - 2))
                        pe.wait_ge(S("h_lo"), T("h_lo", K, c - 2))
                        pe.wait_ge(S("t"), T("t", K, c - 3))
                        (eh, el), (hh, hl) = ([v[:, c % 2] for v in pair] for pair in (eTs, h))
                        pe.matmul(bC[:, 0:D + 2], eh, hh, start=True, stop=False)
                        pe.matmul(bC[:, 0:D], eh, hl[:, 0:D], start=False, stop=False)
                        pe.matmul(bC[:, 0:D + 2], el, hh, start=False, stop=True).then_inc(S("ctx"), 1)
                    if c % 2 == 0 and is_live(K, c):
                        pair_product(K, c, 1)
                        pair_product(K, c, 2)
                    if is_live(K, c):
                        xh, xl = xT_of(c)
                        pe.wait_ge(S("h_lo"), T("h_lo", K, c - 1))
                        pe.matmul(bH[:, 0:D], core.ones[:, :], core.bias[:, bias], start=True, stop=False)
                        for kt in range(KT):
                            last = mm3(pe, bH[:, 0:D], [xh[:, kt], xl[:, kt]], [wh[:, 2, kt], wl[:, 2, kt]],
                                       False, kt == KT - 1)
                        last.then_inc(S("h_ps"), 1)
                        pe.wait_ge(S("g_lo"), P2("g_lo", K, c, per=KT))
                        pe.wait_ge(S("w"), T("w", K, c - 1))
                        for kt in range(KT):
                            last = mm3(pe, bU[:, 0:2 * N].rearrange("p (a b) -> p a b", a=2), [xh[:, kt], xl[:, kt]],
                                       [v[:, kt::KT, c % 2] for v in g], kt == 0, kt == KT - 1)
                        last.then_inc(S("u_ps"), 1)
                    if is_live(K, c + 1):
                        pe.wait_ge(S(f"adjacency{(c + 1) % U}"), B("adjacency", K, c + 1, U, 16))
                        pe.wait_ge(S("adjT"), T("adjT", K, c))
                        pe.transpose(bA[:, 0:N], adj[:, (c + 1) % U], core.ident[:, :]).then_inc(S("adjT_ps"), 1)
                    if is_live(K, c + 3):
                        pe.wait_ge(S(f"loaded{(c + 3) % U}"), B("loaded", K, c + 3, U, 16))
                        pe.wait_ge(S("xT_lo"), T("xT_lo", K, c + 2))
                        for kt in range(KT):
                            last = pe.transpose(bT[:, kt * N:(kt + 1) * N], x[:, (c + 3) % U, kt * 128:(kt + 1) * 128],
                                                core.ident[:, :])
                        last.then_inc(S("xT_ps"), 1)
                steps(pe, body, 2, head=3)

            @block.scalar
            def _(act):
                def g_hi(K, c, j):
                    if is_live(K, c):
                        act.wait_ge(S("g_ps"), P2("g_ps", K, c, per=KT, extra=j - 2))
                        act.activation(chunk(g[0], j), bG[j][:, :], ACT.Copy).then_inc(S("g_hi"), 1)

                def h_hi(K, c):
                    if is_live(K, c):
                        act.wait_ge(S("h_ps"), T("h_ps", K, c))
                        act.activation(h[0][:, c % 2, 0:D], bH[:, 0:D], ACT.Copy).then_inc(S("h_hi"), 1)

                def body(K, c):
                    core.next_split(act, core.split_hi, n, K, c)
                    if c % 2 == 0:
                        g_hi(K, c, 0)
                    if is_live(K, c - 1):
                        act.wait_ge(S("u"), T("u", K, c - 1))
                        act.activation(e[:, :], u[:, :], ACT.Exp, scale=temper).then_inc(S("exp"), 1)
                    if c % 2 == 0:
                        g_hi(K, c, 1)
                    if is_live(K, c - 1):
                        act.wait_ge(S("ea"), T("ea", K, c - 1))
                        act.activation(eTs[0][:, (c - 1) % 2], ea[:, :], ACT.Copy).then_inc(S("eT_hi"), 1)
                    if c % 2 == 0:
                        g_hi(K, c, 2)
                        h_hi(K, c)
                    if is_live(K, c - 2):
                        act.wait_ge(S("nq"), T("nq", K, c - 2))
                        act.activation(t[:, c % 2], bC[:, 0:D], ACT.Identity, bias=col(c, NQ), scale=col(c, Q))\
                            .then_inc(S("t"), 1)
                    if c % 2 == 1:
                        h_hi(K, c)
                    if is_live(K, c + 1):
                        act.wait_ge(S("adjT_ps"), T("adjT_ps", K, c + 1))
                        act.activation(adjT[:, (c + 1) % 2], bA[:, 0:N], ACT.Copy).then_inc(S("adjT"), 1)
                    if is_live(K, c + 3):
                        act.wait_ge(S("xT_ps"), T("xT_ps", K, c + 3))
                        act.activation(xT_of(c + 3)[0], tiles(bT), ACT.Copy).then_inc(S("xT_hi"), 1)
                    if is_live(K, c - 3) and closing:
                        act.wait_ge(S("nmr2"), T("nmr2", K, c - 3))
                        act.wait_ge(S(f"stored{(c - 5) % 2}"), B("stored", K, c - 5, 2, 16))
                        act.activation(o[:, (c - 3) % 2], y[:, (c - 3) % 2], ACT.Identity, bias=col(c - 3, NMR2),
                                       scale=col(c - 3, RSTD2)).then_inc(S("o"), 1)
                steps(act, body, 3, head=3)

            @block.gpsimd
            def _(pool):
                def body(K, c):
                    core.next_split(pool, core.split_lo, n, K, c)
                    if is_live(K, c):
                        pool.wait_ge(S(f"adjacency{c % U}"), B("adjacency", K, c, U, 16))
                        pool.wait_ge(S("w"), T("w", K, c - 2))
                        pool.tensor_tensor(mask[:, c % 2, 1], adj[:, c % U], core.upper[:, :], ALU.mult).then_inc(S("mask_r"), 1)
                        pool.wait_ge(S("adjT"), T("adjT", K, c))
                        pool.tensor_tensor(mask[:, c % 2, 0], adjT[:, c % 2], core.lowtri[:, :], ALU.mult).then_inc(S("mask_l"), 1)
                    if is_live(K, c - 2):
                        pool.wait_ge(S("agg"), T("agg", K, c - 2))
                        pool.tensor_tensor(col(c, VE), col(c, AG + 1), core.scalar(UNBIASED), ALU.mult).then_inc(S("var1"), 1)
                        pool.wait_ge(S("var1"), T("var1", K, c - 2))
                        pool.tensor_tensor(col(c, SD), col(c, VE), core.scalar(SQRT), ALU.pow).then_inc(S("sigma"), 1)
                    if is_live(K, c - 1):
                        pool.wait_ge(S("eT_hi"), T("eT_hi", K, c - 1))
                        pool.tensor_tensor(eTs[1][:, (c - 1) % 2], ea[:, :], eTs[0][:, (c - 1) % 2].bitcast(fp32), ALU.subtract).then_inc(S("eT_lo"), 1)
                    if is_live(K, c - 3) and closing:
                        pool.wait_ge(S("agg2"), T("agg2", K, c - 3))
                        pool.tensor_tensor(col(c - 3, VE2), col(c - 3, AG2 + 1), core.scalar(EPS_OUTER), ALU.add).then_inc(S("veps2"), 1)
                        pool.wait_ge(S("veps2"), T("veps2", K, c - 3))
                        pool.tensor_tensor(col(c - 3, RSTD2), col(c - 3, VE2), core.scalar(INV_SQRT), ALU.pow).then_inc(S("rstd2"), 1)
                    if is_live(K, c - 2):
                        pool.wait_ge(S("t"), T("t", K, c - 2))
                        tt = t[:, c % 2]
                        pool.tensor_tensor(tt, tt, core.gain[:, gain], ALU.mult).then_inc(S("gained"), 1)
                        pool.wait_ge(S("gained"), T("gained", K, c - 2))
                        pool.tensor_tensor(tt, tt, core.gain[:, gain + 1], ALU.add).then_inc(S("shifted"), 1)
                steps(pool, body, 3, head=2)

            @block.vector
            def _(dve):
                dve.memset(h[0][:, :, D:D + 2].bitcast(fp32), 1.0).then_inc(core.sem("ones_columns"), 1)

                def masked(K, c):
                    if is_live(K, c - 1):
                        dve.wait_ge(S("exp"), T("exp", K, c - 1))
                        dve.wait_ge(S("adjT"), T("adjT", K, c - 1))
                        dve.wait_ge(S("eT_lo"), T("eT_lo", K, c - 2))
                        dve.tensor_tensor(ea[:, :], e[:, :], adjT[:, (c - 1) % 2], ALU.mult).then_inc(S("ea"), 1)

                def ctx_stats(K, c):
                    if is_live(K, c - 2):
                        dve.wait_ge(S("ctx"), T("ctx", K, c - 2))
                        dve.bn_stats(col(c, ST, 6), bC[:, 0:D]).then_inc(S("bn"), 1)

                def ctx_moments(K, c):
                    if is_live(K, c - 2):
                        dve.wait_ge(S("bn"), T("bn", K, c - 2))
                        dve.tensor_scalar(col(c, RS), bC[:, D:D + 1], 1e-10, None, ALU.add).then_inc(S("rsum"), 1)
                        dve.bn_aggr(col(c, AG, 2), col(c, ST, 6)).then_inc(S("agg"), 1)

                def g_lo(K, c, j):
                    dve.wait_ge(S("g_hi"), P2("g_hi", K, c, per=KT, extra=j - 2))
                    dve.tensor_tensor(chunk(g[1], j), bG[j][:, :], chunk(g[0], j).bitcast(fp32),
                                      ALU.subtract).then_inc(S("g_lo"), 1)

                def body(K, c):
                    if is_live(K, c - 1):
                        dve.wait_ge(S("u_ps"), T("u_ps", K, c - 1))
                        dve.wait_ge(S("mask_l"), T("mask_l", K, c - 1))
                        dve.tensor_tensor(w[:, :, :], bU[:, 0:2 * N].rearrange("p (a b) -> p a b", a=2),
                                          mask[:, (c - 1) % 2], ALU.mult).then_inc(S("w"), 1)
                        dve.wait_ge(S("w"), T("w", K, c - 1))
                        dve.tensor_tensor(u[:, :], w[:, 0], w[:, 1], ALU.add).then_inc(S("u"), 1)
                    if c % 2 == 1:
                        ctx_stats(K, c)
                    else:
                        if is_live(K, c):
                            g_lo(K, c, 0)
                        masked(K, c)
                    if is_live(K, c - 3):
                        dve.wait_ge(S("shifted"), T("shifted", K, c - 3))
                        if closing:
                            dve.wait_ge(S(f"residual{(c - 3) % U}"), B("residual", K, c - 3, U, 16))
                            dve.scalar_tensor_tensor(y[:, (c - 3) % 2], t[:, (c - 3) % 2], 0.0, res[:, (c - 3) % U],
                                                     op0=ALU.max, op1=ALU.add).then_inc(S("y"), 1)
                        else:
                            dve.wait_ge(S(f"stored{(c - 5) % 2}"), B("stored", K, c - 5, 2, 16))
                            dve.tensor_scalar(y[:, (c - 3) % 2], t[:, (c - 3) % 2], 0.0, None, ALU.max).then_inc(S("y"), 1)
                    if c % 2 == 1:
                        ctx_moments(K, c)
                    if c % 2 == 1:
                        masked(K, c)
                    if c % 2 == 0:
                        ctx_stats(K, c)
                        if is_live(K, c):
                            g_lo(K, c, 1)
                        ctx_moments(K, c)
                    if is_live(K, c - 3) and closing:
                        dve.wait_ge(S("y"), T("y", K, c - 3))
                        dve.bn_stats(col(c - 3, ST2, 6), y[:, (c - 3) % 2]).then_inc(S("bn2"), 1)
                    if c % 2 == 0 and is_live(K, c):
                        g_lo(K, c, 2)
                    if is_live(K, c - 3) and closing:
                        dve.wait_ge(S("bn2"), T("bn2", K, c - 3))
                    if is_live(K, c - 2):
                        dve.wait_ge(S("rsum"), T("rsum", K, c - 2))
                        dve.wait_ge(S("sigma"), T("sigma", K, c - 2))
                        dve.scalar_tensor_tensor(col(c, DEN), col(c, RS), 1e-3, col(c, SD), op0=ALU.mult, op1=ALU.add)\
                            .then_inc(S("den"), 1)
                    if is_live(K, c - 3) and closing:
                        dve.bn_aggr(col(c - 3, AG2, 2), col(c - 3, ST2, 6)).then_inc(S("agg2"), 1)
                    if is_live(K, c - 2):
                        dve.wait_ge(S("den"), T("den", K, c - 2))
                        dve.reciprocal(col(c, Q), col(c, DEN)).then_inc(S("q"), 1)
                        dve.wait_ge(S("q"), T("q", K, c - 2))
                        dve.scalar_tensor_tensor(col(c, NQ), col(c, AG), -1.0, col(c, Q), op0=ALU.mult, op1=ALU.mult)\
                            .then_inc(S("nq"), 1)
                    if is_live(K, c):
                        dve.wait_ge(S("h_hi"), T("h_hi", K, c))
                        dve.tensor_tensor(h[1][:, c % 2, 0:D], bH[:, 0:D], h[0][:, c % 2, 0:D].bitcast(fp32),
                                          ALU.subtract).then_inc(S("h_lo"), 1)
                    if is_live(K, c - 3) and closing:
                        dve.wait_ge(S("rstd2"), T("rstd2", K, c - 3))
                        dve.scalar_tensor_tensor(col(c - 3, NMR2), col(c - 3, AG2), -1.0, col(c - 3, RSTD2), op0=ALU.mult,
                                                 op1=ALU.mult).then_inc(S("nmr2"), 1)
                    if is_live(K, c + 3):
                        dve.wait_ge(S("xT_hi"), T("xT_hi", K, c + 3))
                        dve.tensor_tensor(xT_of(c + 3)[1], tiles(bT), xT_of(c + 3)[0].bitcast(fp32), ALU.subtract)\
                            .then_inc(S("xT_lo"), 1)
                steps(dve, body, 3, head=3)


def attention(core, n, src, dst):
    nc = core.nc
    ph = Phase(core, n)
    S, T, P2, B = ph.sem, ph.upto, ph.pairs, ph.moved
    scale = float(D) ** -0.5
    R = 128 // HEAD
    wh, wl = core.w_hi[:, n % 2], core.w_lo[:, n % 2]
    banks = core.banks
    bV, bT, bOT, bY, bO = banks[3:8]
    QK = 2 * KT
    with ExitStack() as lc:
        sb = lambda name, shape, dt=fp32: lc.enter_context(nc.sbuf_tensor(f"{name}_{n}", shape, dt))
        x = sb("x", [128, U, D])
        res = sb("res", [128, U, D])
        adj = sb("adj", [128, U, N])
        xT = [sb(f"xT{i}", [128, 2, KT, 2, N], fp32r) for i in "hl"]
        qk = sb("qk", [128, QK, 2, N])
        v = sb("v", [128, U, HEADS, HV])
        a = sb("a", [128, HEADS, N])
        e = sb("e", [128, HEADS, N])
        eT = sb("eT", [128, HEADS, N])
        att = sb("att", [128, KT, R, HEAD])
        oT = [sb(f"oT{i}", [128, KT, N], fp32r) for i in "hl"]
        y = sb("y", [128, 2, D])
        o = sb("o", [128, 2, D])
        hs = sb("hs", [128, 2, 6, HEADS])
        MX, MN, NZ, KEEP, RI, RK = range(6)
        sm = sb("sm", [128, 2, 16])
        ST2, AG2, VE2, RSTD2, NMR2 = 0, 6, 8, 9, 10

        def col(c, i, w=1):
            return sm[:, c % 2, i:i + w]

        def xT_of(c):
            return [t[:, c // 2 % 2, :, c % 2] for t in xT]

        def tiles(bank):
            return bank[:, 0:D].rearrange("p (a b) -> p a b", a=KT)

        def chunk(j):
            return qk[:, 2 * j:2 * j + 2].rearrange("p a b c -> p (a b c)")

        def grouped(tile):
            return tile.rearrange("p (r t) d -> p r t d", r=R)

        with nc.Block() as block:
            @block.sync
            def _(sp):
                core.load_weights(sp, n + 1)

                def body(K, c):
                    if is_live(K, c - 5):
                        sp.wait_ge(S("o"), T("o", K, c - 5))
                        sp.dma_start(tile_of(dst, K, c - 5), o[:, (c - 5) % 2]).then_inc(S(f"stored{(c - 5) % 2}"), 16)
                    if is_live(K, c + 3):
                        sp.wait_ge(S("xT_ps"), T("xT_ps", K, c + 3 - U))
                        sl = (c + 3) % U
                        sp.dma_start(x[:, sl], tile_of(src, K, c + 3)).then_inc(S(f"loaded{sl}"), 16)
                    if is_live(K, c + 2):
                        sp.wait_ge(S("a_parts"), T("a_parts", K, c + 2 - U, per=R))
                        sl = (c + 2) % U
                        sp.dma_start(adj[:, sl], tile_of(core.adj_in, K, c + 2)).then_inc(S(f"adjacency{sl}"), 16)
                    if is_live(K, c):
                        sp.wait_ge(S("y"), T("y", K, c - U))
                        sl = c % U
                        sp.dma_start(res[:, sl], tile_of(src, K, c)).then_inc(S(f"residual{sl}"), 16)
                steps(sp, body, 5, head=3)
                for i in range(2):
                    sp.wait_ge(S(f"stored{i}"), T(f"stored{i}", LAST, U - 1) * 8)

            @block.tensor
            def _(pe):
                for m in range(4):
                    pe.wait_ge(core.sem(f"w_lo{m}"), core.uses(n, m))
                pe.wait_ge(core.sem("ones_columns"), n)

                def pair_product(K, c, j):
                    if j == 1:
                        pe.wait_ge(S("oT_lo"), T("oT_lo", K, c - 3))
                    if j == 2:
                        pe.wait_ge(S("y"), T("y", K, c - 4))
                    for k in (2 * j, 2 * j + 1):
                        cols = slice(k % KT * 128, (k % KT + 1) * 128)
                        for kt in range(KT):
                            last = mm3(pe, banks[4 + j][:, k % 2 * 2 * N:(k % 2 + 1) * 2 * N],
                                       [wh[:, k // KT, kt, cols], wl[:, k // KT, kt, cols]],
                                       [t[:, c // 2 % 2, kt].rearrange("p a b -> p (a b)") for t in xT],
                                       kt == 0, kt == KT - 1)
                    last.then_inc(S("qk_ps"), 1)

                def product(bank, row, m, lhs, k):
                    if k == 0:
                        return pe.matmul(bank[:, 0:D], core.ones[:, :], core.bias[:, row], start=True, stop=False)
                    kt, (p, q) = (k - 1) // 3, ((0, 0), (0, 1), (1, 0))[(k - 1) % 3]
                    return pe.matmul(bank[:, 0:D], lhs[p][:, kt], (wh, wl)[q][:, m, kt],
                                     start=row is None and k == 1, stop=k == 9)

                def value_product(K, c, k):
                    if k == 0:
                        pe.wait_ge(S("a_parts"), T("a_parts", K, c - 1, per=R))
                    last = product(bV, 3, 2, xT_of(c), k)
                    if k == 9:
                        last.then_inc(S("v_ps"), 1)

                def output_product(K, c, k):
                    if k == 1:
                        pe.wait_ge(S("oT_lo"), T("oT_lo", K, c - 3))
                        pe.wait_ge(S("y"), T("y", K, c - 4))
                        pe.wait_ge(S("qk_act"), P2("qk_act", K, c, per=2))
                    last = product(bY, None, 3, oT, k)
                    if k == 9:
                        last.then_inc(S("y_ps"), 1)

                def head_product(K, c, i):
                    if i == 0:
                        pe.wait_ge(S("v"), T("v", K, c - 2))
                        pe.wait_ge(S("att"), T("att", K, c - 3))
                    if i % 4 == 0:
                        pe.wait_ge(S("eT_parts"), T("eT_parts", K, c - 2, per=KT, extra=i // 4 - 2))
                    last = pe.matmul(bO[:, i * HV:(i + 1) * HV], eT[:, i], v[:, (c - 2) % U, i], start=True, stop=True)
                    if i == HEADS - 1:
                        last.then_inc(S("av"), 1)

                def score_product(K, c, i):
                    if i == 0:
                        pe.wait_ge(S("qk_act"), P2("qk_act", K, c, per=2))
                        pe.wait_ge(S("qk_dve"), P2("qk_dve", K, c))
                        pe.wait_ge(S("eT_parts"), T("eT_parts", K, c - 2, per=KT))
                    if i == (R - 1) * KT:
                        pe.wait_ge(S("v"), T("v", K, c))
                    r, ct = i // KT, i % KT
                    rows = slice(r * HEAD, (r + 1) * HEAD)
                    last = pe.matmul(banks[r][:, ct * N:(ct + 1) * N], qk[rows, ct, c % 2],
                                     qk[rows, KT + ct, c % 2], start=True, stop=True)
                    if ct == KT - 1:
                        last.then_inc(S("scores_parts"), 1)

                def body(K, c):
                    new_pair = c % 2 == 0 and is_live(K, c)
                    if new_pair:
                        pe.wait_ge(S("xT_lo"), T("xT_lo", K, c + 1))
                        pair_product(K, c, 0)
                    if is_live(K, c - 2):
                        pe.wait_ge(S("exp"), T("exp", K, c - 2))
                        for b in range(KT):
                            pe.wait_ge(S("a_parts"), T("a_parts", K, c - 1, per=R, extra=b - 3))
                            for i in range(4):
                                last = pe.transpose(banks[b][:, i * N:(i + 1) * N], e[:, 4 * b + i], core.ident[:, :])
                            last.then_inc(S("eT_ps_parts"), 1)
                    if new_pair:
                        pair_product(K, c, 1)
                        pair_product(K, c, 2)
                    for k in range(HEADS + 2):
                        if is_live(K, c) and k < 10:
                            value_product(K, c, k)
                        if is_live(K, c - 2) and k >= 2:
                            head_product(K, c, k - 2)
                    if is_live(K, c + 2):
                        pe.wait_ge(S(f"loaded{(c + 2) % U}"), B("loaded", K, c + 2, U, 16))
                        pe.wait_ge(S("xT_lo"), T("xT_lo", K, c + 1))
                        pe.wait_ge(S("qk_act"), P2("qk_act", K, c, per=2))
                        for kt in range(KT):
                            last = pe.transpose(bT[:, kt * N:(kt + 1) * N], x[:, (c + 2) % U, kt * 128:(kt + 1) * 128],
                                                core.ident[:, :])
                        last.then_inc(S("xT_ps"), 1)
                    for k in range(HEADS):
                        if is_live(K, c):
                            score_product(K, c, k)
                        if is_live(K, c - 3) and k < 9:
                            output_product(K, c, k + 1)
                    if is_live(K, c - 2):
                        pe.wait_ge(S("att"), T("att", K, c - 2))
                        pe.wait_ge(S("oT_lo"), T("oT_lo", K, c - 3))
                        pe.wait_ge(S("qk_dve"), P2("qk_dve", K, c))
                        for kt in range(KT):
                            last = pe.transpose(bOT[:, kt * N:(kt + 1) * N], att[:, kt].rearrange("p r d -> p (r d)"),
                                                core.ident[:, :])
                        last.then_inc(S("oT_ps"), 1)
                steps(pe, body, 3, head=2)

            @block.scalar
            def _(act):
                def body(K, c):
                    core.next_split(act, core.split_hi, n, K, c)
                    if c % 2 == 0 and is_live(K, c):
                        act.wait_ge(S("qk_ps"), P2("qk_ps", K, c, per=KT, extra=-2))
                        act.activation(chunk(0), banks[4][:, :], ACT.Copy).then_inc(S("qk_act"), 1)
                    if is_live(K, c - 2):
                        for b in range(KT):
                            act.wait_ge(S("eT_ps_parts"), T("eT_ps_parts", K, c - 2, per=KT, extra=b - 2))
                            act.activation(eT[:, 4 * b:4 * b + 4], banks[b][:, :].rearrange("p (a b) -> p a b", a=4),
                                           ACT.Copy).then_inc(S("eT_parts"), 1)
                    if c % 2 == 0 and is_live(K, c):
                        act.wait_ge(S("qk_ps"), P2("qk_ps", K, c, per=KT))
                        act.activation(chunk(2), banks[6][:, :], ACT.Copy).then_inc(S("qk_act"), 1)
                    if is_live(K, c):
                        act.wait_ge(S("v_ps"), T("v_ps", K, c))
                        act.activation(grouped(v[:, c % U, :, 0:HEAD]), bV[:, 0:D].rearrange("p (t r d) -> p r t d", t=KT, r=R),
                                       ACT.Copy).then_inc(S("v"), 1)
                    if is_live(K, c + 2):
                        act.wait_ge(S("xT_ps"), T("xT_ps", K, c + 2))
                        act.activation(xT_of(c + 2)[0], tiles(bT), ACT.Copy).then_inc(S("xT_hi"), 1)
                    if is_live(K, c - 1):
                        act.wait_ge(S("less_max"), T("less_max", K, c - 1))
                        act.activation(e[:, :, :], e[:, :, :], ACT.Exp).then_inc(S("exp"), 1)
                    if is_live(K, c - 4):
                        act.wait_ge(S("nmr2"), T("nmr2", K, c - 4))
                        act.wait_ge(S(f"stored{(c - 6) % 2}"), B("stored", K, c - 6, 2, 16))
                        act.activation(o[:, (c - 4) % 2], y[:, (c - 4) % 2], ACT.Identity, bias=col(c - 4, NMR2),
                                       scale=col(c - 4, RSTD2)).then_inc(S("o"), 1)
                    if is_live(K, c - 2):
                        act.wait_ge(S("oT_ps"), T("oT_ps", K, c - 2))
                        act.activation(oT[0][:, :, :], tiles(bOT), ACT.Copy).then_inc(S("oT_hi"), 1)
                steps(act, body, 4, head=2)

            @block.gpsimd
            def _(pool):
                def body(K, c):
                    core.next_split(pool, core.split_lo, n, K, c)
                    if is_live(K, c - 1):
                        pool.wait_ge(S("max"), T("max", K, c - 1))
                        pool.wait_ge(S("eT_ps_parts"), T("eT_ps_parts", K, c - 2, per=KT))
                        pool.tensor_tensor(e[:, :, :], a[:, :, :],
                                           hs[:, (c - 1) % 2, MX].unsqueeze(2).to_broadcast([128, HEADS, N]),
                                           ALU.subtract).then_inc(S("less_max"), 1)
                    if is_live(K, c - 3):
                        pool.wait_ge(S(f"residual{(c - 3) % U}"), B("residual", K, c - 3, U, 16))
                        pool.tensor_tensor(res[:, (c - 3) % U], res[:, (c - 3) % U], core.gain[:, NG - 1], ALU.add)\
                            .then_inc(S("with_bias"), 1)
                    if is_live(K, c - 4):
                        pool.wait_ge(S("agg2"), T("agg2", K, c - 4))
                        pool.tensor_tensor(col(c - 4, VE2), col(c - 4, AG2 + 1), core.scalar(EPS_OUTER), ALU.add).then_inc(S("veps2"), 1)
                        pool.wait_ge(S("veps2"), T("veps2", K, c - 4))
                        pool.tensor_tensor(col(c - 4, RSTD2), col(c - 4, VE2), core.scalar(INV_SQRT), ALU.pow).then_inc(S("rstd2"), 1)
                steps(pool, body, 4)

            @block.vector
            def _(dve):
                dve.memset(v[:, :, :, HEAD:HV], 1.0).then_inc(core.sem("ones_columns"), 1)

                def body(K, c):
                    if is_live(K, c - 4):
                        dve.wait_ge(S("y_ps"), T("y_ps", K, c - 4))
                        dve.wait_ge(S("with_bias"), T("with_bias", K, c - 4))
                        dve.tensor_tensor(y[:, (c - 4) % 2], bY[:, 0:D], res[:, (c - 4) % U], ALU.add).then_inc(S("y"), 1)
                    m = hs[:, (c - 1) % 2]
                    if is_live(K, c - 1):
                        dve.wait_ge(S("max"), T("max", K, c - 1))
                        dve.tensor_scalar(m[:, NZ], m[:, MX], 0.0, None, ALU.not_equal).then_inc(S("nonzero"), 1)
                    if is_live(K, c - 4):
                        dve.wait_ge(S("y"), T("y", K, c - 4))
                        dve.bn_stats(col(c - 4, ST2, 6), y[:, (c - 4) % 2]).then_inc(S("bn2"), 1)
                    if is_live(K, c - 1):
                        dve.tensor_reduce(m[:, MN], a[:, :, :], AX.X, ALU.min).then_inc(S("min"), 1)
                    if is_live(K, c - 4):
                        dve.wait_ge(S("bn2"), T("bn2", K, c - 4))
                    if is_live(K, c - 1):
                        dve.wait_ge(S("min"), T("min", K, c - 1))
                        dve.wait_ge(S("nonzero"), T("nonzero", K, c - 1))
                        dve.scalar_tensor_tensor(m[:, KEEP], m[:, MN], 0.0, m[:, NZ], op0=ALU.not_equal, op1=ALU.max)\
                            .then_inc(S("keep"), 1)
                    if is_live(K, c - 4):
                        dve.bn_aggr(col(c - 4, AG2, 2), col(c - 4, ST2, 6)).then_inc(S("agg2"), 1)
                    if c % 2 == 0 and is_live(K, c):
                        dve.wait_ge(S("qk_ps"), P2("qk_ps", K, c, per=KT, extra=-1))
                        dve.tensor_copy(chunk(1), banks[5][:, :]).then_inc(S("qk_dve"), 1)
                    if is_live(K, c - 4):
                        dve.wait_ge(S("rstd2"), T("rstd2", K, c - 4))
                        dve.scalar_tensor_tensor(col(c - 4, NMR2), col(c - 4, AG2), -1.0, col(c - 4, RSTD2), op0=ALU.mult,
                                                 op1=ALU.mult).then_inc(S("nmr2"), 1)
                    if is_live(K, c - 2):
                        dve.wait_ge(S("av"), T("av", K, c - 2))
                        m = hs[:, c % 2]
                        heads = bO[:, 0:HEADS * HV].rearrange("p (h d) -> p h d", h=HEADS)
                        dve.reciprocal(m[:, RI], heads[:, :, HEAD]).then_inc(S("rinv"), 1)
                        dve.wait_ge(S("rinv"), T("rinv", K, c - 2))
                        dve.wait_ge(S("keep"), T("keep", K, c - 2))
                        dve.tensor_tensor(m[:, RK], m[:, RI], m[:, KEEP], ALU.mult).then_inc(S("rkeep"), 1)
                        dve.wait_ge(S("rkeep"), T("rkeep", K, c - 2))
                        dve.tensor_tensor(att[:, :, :, :].rearrange("p t r d -> p r t d"), grouped(heads[:, :, 0:HEAD]),
                                          grouped(m[:, RK].unsqueeze(2).to_broadcast([128, HEADS, HEAD])), ALU.mult)\
                            .then_inc(S("att"), 1)
                    if is_live(K, c + 2):
                        dve.wait_ge(S("xT_hi"), T("xT_hi", K, c + 2))
                        dve.tensor_tensor(xT_of(c + 2)[1], tiles(bT), xT_of(c + 2)[0].bitcast(fp32), ALU.subtract)\
                            .then_inc(S("xT_lo"), 1)
                    if is_live(K, c):
                        dve.wait_ge(S("less_max"), T("less_max", K, c - 1))
                        dve.wait_ge(S(f"adjacency{c % U}"), B("adjacency", K, c, U, 16))
                        for r in range(R):
                            dve.wait_ge(S("scores_parts"), T("scores_parts", K, c, per=R, extra=r - 3))
                            dve.scalar_tensor_tensor(a[:, KT * r:KT * (r + 1)], tiles(banks[r]), scale,
                                                     adj[:, c % U].unsqueeze(1).to_broadcast([128, KT, N]),
                                                     op0=ALU.mult, op1=ALU.add).then_inc(S("a_parts"), 1)
                    if is_live(K, c - 2):
                        dve.wait_ge(S("oT_hi"), T("oT_hi", K, c - 2))
                        dve.tensor_tensor(oT[1][:, :, :], tiles(bOT), oT[0][:, :, :].bitcast(fp32),
                                          ALU.subtract).then_inc(S("oT_lo"), 1)
                    if is_live(K, c):
                        dve.wait_ge(S("a_parts"), T("a_parts", K, c, per=R))
                        dve.reduce_max(hs[:, c % 2, MX], a[:, :, :], AX.X).then_inc(S("max"), 1)
                steps(dve, body, 4, head=2)


def kernel(**inputs):
    import numpy as _np
    import concourse.bacc as _bacc
    from concourse import mybir as _mybir
    from concourse.bass_utils import run_bass_kernel_spmd as _run

    i = {k: _np.ascontiguousarray(v) for k, v in inputs.items()}
    mats = [i["L0_gnn_W_left"].T, i["L0_gnn_W_self"].T, i["L0_gnn_W_right"].T,
            i["L1_gnn_Wq"].T, i["L1_gnn_Wk"].T, i["L1_gnn_Wv"].T, i["L1_gnn_Wo"].T]
    for l in range(2):
        mats += [i["L2_gnn_W_left"][l], i["L2_gnn_W_right"][l], i["L2_gnn_W_lin"][l].T]
    for l in range(2):
        mats += [i["L3_gnn_Wl"][l].T, i["L3_gnn_Ws"][l].T, i["L3_gnn_Wr"][l].T]
    w = _np.ascontiguousarray(_np.stack(mats).reshape(len(mats), KT, 128, D).transpose(0, 2, 1, 3))
    rows = [i["L0_gnn_b_left"], i["L0_gnn_b_self"], i["L0_gnn_b_right"], i["L1_gnn_bv"], i["L1_gnn_bo"],
            i["L2_gnn_b_lin"][0], i["L2_gnn_b_lin"][1]]
    for l in range(2):
        rows += [i["L3_gnn_bl"][l], i["L3_gnn_bs"][l], i["L3_gnn_br"][l]]
    gains = [i["L0_gnn_gamma"], i["L0_gnn_beta"]]
    for l in range(2):
        gains += [i["L2_gnn_ln_a"][l], i["L2_gnn_ln_b"][l]]
    for l in range(2):
        gains += [i["L3_gnn_ln_w"][l], i["L3_gnn_ln_b"][l]]
    gains += [i["L1_gnn_bo"]]
    arrays = {"x": i["x"], "adj": i["adj"], "weights": w, "bias_rows": _np.stack(rows), "gain_rows": _np.stack(gains)}

    nc = _bacc.Bacc("TRN2", target_bir_lowering=False, num_devices=1)
    args = [nc.dram_tensor(k, a.shape, _mybir.dt.from_np(a.dtype), kind="ExternalInput").ap() for k, a in arrays.items()]
    out = nc.dram_tensor("out", (G, N, D), _mybir.dt.float32, kind="ExternalOutput").ap()
    scratch = [nc.dram_tensor(f"scratch{k}", (G, N, D), _mybir.dt.float32, kind="Internal").ap() for k in range(5)]
    program(nc, *args, out, scratch)
    r = _run(nc, [arrays], core_ids=[0])
    return r.results[0]["out"]
```
